# Optimizing a Trainium2 kernel written in Bass

```python
import numpy as np
import jax
import jax.numpy as jnp

def _softmax(x, axis=-1):
    return jax.nn.softmax(x, axis=axis)

def _gelu(x):
    return jax.nn.gelu(x, approximate=True)

def _silu(x):
    return jax.nn.silu(x)

def _sigmoid(x):
    return jax.nn.sigmoid(x)

def _layernorm(x, axis=-1, eps=1e-05):
    m = jnp.mean(x, axis=axis, keepdims=True)
    v = jnp.var(x, axis=axis, keepdims=True)
    return (x - m) / jnp.sqrt(v + eps)

def _scatter_add(tgt, idx, src, axis=0):
    return tgt.at[idx].add(src)

def _segment_sum(src, seg, n):
    return jax.ops.segment_sum(src, seg, n)
kernel_name = 'mk_adj_ffn_d1_adj_r2_ba0770'

def setup_inputs(seed: int=0):
    np.random.seed(seed)
    _w = jnp.asarray

    def _rec_inputs():
        import jax
        import jax.numpy as jnp
        _gk = jax.random.key(seed)
        x = 0.5 + 0.2887 * jax.random.normal(jax.random.fold_in(_gk, 1), (2048, 512), jnp.float32)
        _a = jax.random.bernoulli(jax.random.fold_in(_gk, 2), 0.000976562, (2048, 2048))
        _a = jnp.logical_or(_a, jnp.eye(2048, dtype=bool))
        _af = _a.astype(jnp.float32)
        _af = _af * jax.random.uniform(jax.random.fold_in(_gk, 3), (2048, 2048), jnp.float32, 0.05, 1)
        adj = _af
        return (x, adj)
    x, adj = _rec_inputs()

    def _L0_gnn_setup():
        import jax, jax.numpy as jnp
        import numpy as np
        NBITS = 4
        N_NODES = 4096
        IN_F = 512
        OUT_F = 512

        def _act_quant(x, alpha, b):
            n = float(2 ** b - 1)
            xd = x / alpha
            xc = jnp.minimum(xd, 1.0)
            xq = jnp.round(xc * n) / n
            return xq * alpha

        def _weight_quant(w, alpha, b):
            n = float(2 ** b - 1)
            wd = w / alpha
            wc = jnp.clip(wd, -1.0, 1.0)
            wq = jnp.round(jnp.abs(wc) * n) / n * jnp.sign(wc)
            return wq * alpha
        key = jax.random.key(seed)
        k1, k2, k3 = jax.random.split(key, 3)
        stdv = 1.0 / np.sqrt(OUT_F)
        inp = {'input': jax.random.uniform(k1, (N_NODES, IN_F), dtype=jnp.float32), 'adj': jax.random.uniform(k2, (N_NODES, N_NODES), dtype=jnp.float32), 'adj_scaling_factor': jnp.float32(2.0), 'weight': jax.random.uniform(k3, (IN_F, OUT_F), minval=-stdv, maxval=stdv, dtype=jnp.float32), 'wgt_alpha': jnp.float32(3.0), 'act_alpha': jnp.float32(1.0), 'act_alpha2': jnp.float32(1.0)}
        return inp
    _L0_gnn_all = _L0_gnn_setup()
    _L0_gnn_in = {k: v for k, v in _L0_gnn_all.items() if k in ('adj_scaling_factor', 'weight', 'wgt_alpha', 'act_alpha', 'act_alpha2')}
    del _L0_gnn_all

    def _L0_ffn_setup():
        import jax, jax.numpy as jnp
        import numpy as np
        B, S, D = (4, 1024, 512)
        E = 8
        F = 2048
        T = B * S
        CAP = 640
        key = jax.random.key(seed)
        k1, k2, k3, k4 = jax.random.split(key, 4)
        inputs = jax.random.normal(k1, (B, S, D), dtype=jnp.float32)
        gate_w = jax.random.normal(k2, (D, E), dtype=jnp.float32) / np.sqrt(D)
        w1 = jax.random.normal(k3, (E, D, F), dtype=jnp.float32) / np.sqrt(D)
        w2 = jax.random.normal(k4, (E, F, D), dtype=jnp.float32) / np.sqrt(F)
        return {'inputs': inputs, 'gate_w': gate_w, 'w1': w1, 'w2': w2}
    _L0_ffn_all = _L0_ffn_setup()
    _L0_ffn_in = {k: v for k, v in _L0_ffn_all.items() if k in ('gate_w', 'w1', 'w2')}
    del _L0_ffn_all
    return {'x': x, 'adj': adj, 'L0_gnn_adj_scaling_factor': _L0_gnn_in['adj_scaling_factor'], 'L0_gnn_weight': _L0_gnn_in['weight'], 'L0_gnn_wgt_alpha': _L0_gnn_in['wgt_alpha'], 'L0_gnn_act_alpha': _L0_gnn_in['act_alpha'], 'L0_gnn_act_alpha2': _L0_gnn_in['act_alpha2'], 'L0_ffn_gate_w': _L0_ffn_in['gate_w'], 'L0_ffn_w1': _L0_ffn_in['w1'], 'L0_ffn_w2': _L0_ffn_in['w2']}

def reference(x, adj, L0_gnn_adj_scaling_factor, L0_gnn_weight, L0_gnn_wgt_alpha, L0_gnn_act_alpha, L0_gnn_act_alpha2, L0_ffn_gate_w, L0_ffn_w1, L0_ffn_w2):
    import jax
    import jax.numpy as jnp

    def _L0_gnn_ref(input, adj, adj_scaling_factor, weight, wgt_alpha, act_alpha, act_alpha2):
        import jax, jax.numpy as jnp
        import numpy as np
        NBITS = 4
        N_NODES = 4096
        IN_F = 512
        OUT_F = 512

        def _act_quant(x, alpha, b):
            n = float(2 ** b - 1)
            xd = x / alpha
            xc = jnp.minimum(xd, 1.0)
            xq = jnp.round(xc * n) / n
            return xq * alpha

        def _weight_quant(w, alpha, b):
            n = float(2 ** b - 1)
            wd = w / alpha
            wc = jnp.clip(wd, -1.0, 1.0)
            wq = jnp.round(jnp.abs(wc) * n) / n * jnp.sign(wc)
            return wq * alpha
        bit = NBITS
        wb = bit - 1
        mean = jax.lax.stop_gradient(jnp.mean(weight))
        std = jax.lax.stop_gradient(jnp.std(weight, ddof=1))
        w_norm = (weight - mean) / std
        weight_q = _weight_quant(w_norm, wgt_alpha, wb)
        x = _act_quant(input, act_alpha, bit)
        wgt_delta = wgt_alpha / (2 ** (bit - 1) - 1)
        act_delta = act_alpha / (2 ** bit - 1)
        support = jnp.matmul(x / act_delta, weight_q / wgt_delta)
        support = support * act_delta * wgt_delta
        support = jax.nn.relu(support)
        support_q = _act_quant(support, act_alpha2, bit)
        support_delta = act_alpha2 / (2 ** bit - 1)
        output = jnp.matmul(adj / adj_scaling_factor, support_q / support_delta)
        return output * adj_scaling_factor * support_delta

    def _L0_ffn_ref(inputs, gate_w, w1, w2):
        import jax, jax.numpy as jnp
        import numpy as np
        B, S, D = (4, 1024, 512)
        E = 8
        F = 2048
        T = B * S
        CAP = 640
        tokens = inputs.reshape(-1, D)
        logits = tokens @ gate_w
        probs = jax.nn.softmax(logits, axis=-1)
        expert_idx = jnp.argmax(probs, axis=-1)
        mask1 = jax.nn.one_hot(expert_idx, E, dtype=tokens.dtype)
        pos = (jnp.cumsum(mask1, axis=0) - 1.0).astype(jnp.int32)
        sec_mask = mask1[:, :, None] * jax.nn.one_hot(pos, CAP, dtype=tokens.dtype)
        combine_weights = probs[:, :, None] * sec_mask
        expert_input = jnp.einsum('tec,td->ecd', sec_mask, tokens)
        h = jax.nn.relu(jnp.einsum('ecd,edf->ecf', expert_input, w1))
        expert_output = jnp.einsum('ecf,efd->ecd', h, w2)
        out = jnp.einsum('tec,ecd->td', combine_weights, expert_output)
        return out.reshape(inputs.shape)
    x = x + _L0_gnn_ref(_layernorm(x, axis=-1), adj, L0_gnn_adj_scaling_factor, L0_gnn_weight, L0_gnn_wgt_alpha, L0_gnn_act_alpha, L0_gnn_act_alpha2)
    x = x + _L0_ffn_ref(_layernorm(x, axis=-1)[None], L0_ffn_gate_w, L0_ffn_w1, L0_ffn_w2)[0]
    return x

_drawn_inputs = setup_inputs


def setup_inputs(seed=0):
    import zlib

    import numpy as np

    out = dict(_drawn_inputs(seed))
    spreads = {}
    factors = {}
    for name, (base, spread) in spreads.items():
        noise = np.random.default_rng([zlib.crc32(name.encode()), seed]).standard_normal(out[name].shape)
        drawn = base * np.exp(spread * noise) if base else spread * noise
        out[name] = jnp.asarray(drawn.astype(out[name].dtype))
    for name, factor in factors.items():
        out[name] = (out[name] * factor).astype(out[name].dtype)
    return out
```

```python
from contextlib import ExitStack

import concourse.bass as bass
from concourse import mybir

P = 128
T, D, E, F, CAP = 2048, 512, 8, 2048, 640
NT = T // P
KD = D // P
NF = F // P
FC = 4
NC = NF // FC
HALF = CAP // 2
SLOT_TILES = [P, P, HALF - 2 * P]
NSEG = len(SLOT_TILES)
MAX_OVER = T // (HALF + 1)
NPT = E + MAX_OVER + 2
COLS = E * 2 * NSEG
WIDTHS = [256, 288, HALF]
ITEM = NT * P
RING = 4
PIECES = 4
PIECE = ITEM // PIECES
MAGIC = 12582912.0
EPS = 1e-5
ACT_N = 15.0
WGT_N = 7.0
STEP_A = 4

ALU = mybir.AluOpType
ACT = mybir.ActivationFunctionType
AX = mybir.AxisListType.X
F32 = mybir.dt.float32
F32R = mybir.dt.float32r
BF16 = mybir.dt.bfloat16
I32 = mybir.dt.int32


class Chain:

    def __init__(self, engine, sem):
        self.engine, self.sem, self.n, self.base = engine, sem, 0, 0

    def done(self, ins):
        ins.then_inc(self.sem, 1)
        self.n += 1

    def wait(self):
        self.engine.wait_ge(self.sem, self.base + self.n)

    def then(self, ins):
        self.done(ins)
        self.wait()


def wait_apart(engine, sem, value, tick):
    engine.wait_ge(sem, value)
    engine.sem_inc(tick, 1)


def gnn_moe_kernel(nc, x_in, adj_in, w_in, scal_in, gate_in, experts_in, out, x1_rows):
    with ExitStack() as ctx:
        def sb(name, shape, dt):
            return ctx.enter_context(nc.sbuf_tensor(name, shape, dt))

        def psum(name):
            return ctx.enter_context(nc.psum_tensor(name, [P, 512], F32))

        def sem(name):
            return ctx.enter_context(nc.semaphore(name))

        raw = sb("raw", [P, RING, ITEM], F32)
        hi = sb("hi", [P, RING, ITEM], F32R)
        lo = sb("lo", [P, RING, ITEM], F32R)
        x = sb("x", [P, NT, D], F32)
        S = sb("S", [P, NT, D], F32R)
        fr = sb("fr", [P, 8 * 512], F32R)
        fb = sb("fb", [P, 3 * NSEG * D + KD * HALF + P - SLOT_TILES[-1]], F32)

        wq = fr[:, 0:KD * D].rearrange("p (k n) -> p k n", k=KD)
        qT_hi = fr[:, 2048:3072].rearrange("p (b n) -> p b n", b=2)
        qT_lo = fr[:, 3072:4096].rearrange("p (b n) -> p b n", b=2)
        wraw = fb[:, 0:KD * D].rearrange("p (k n) -> p k n", k=KD)
        q = fb[:, 2048:3072].rearrange("p (b n) -> p b n", b=2)
        sup = fb[:, 3072:4096].rearrange("p (b n) -> p b n", b=2)
        xn1 = fb[:, 4096:4608]
        xn1T = fb[:, 4608:5120].rearrange("p (k n) -> p k n", k=KD)
        r_hot = S[:, 0:4, :].rearrange("p a b -> p (a b)").rearrange("p (t r) -> p t r", t=NT)
        payload = S[:, 4:9, :].rearrange("p a b -> p (a b)")[:, 0:NT * 3 * COLS] \
            .rearrange("p (t j c) -> p t j c", t=NT, j=3)
        col_hot = fb[:, 0:NT * COLS].rearrange("p (t c) -> p t c", t=NT)
        xT_hi = fr[:, 0:KD * HALF].rearrange("p (k n) -> p k n", k=KD)
        xT_lo = fr[:, KD * HALF:2 * KD * HALF].rearrange("p (k n) -> p k n", k=KD)
        h_hi = fr[:, 8 * HALF:10 * HALF].rearrange("p (b n) -> p b n", b=2)
        h_lo = fr[:, 10 * HALF:12 * HALF].rearrange("p (b n) -> p b n", b=2)
        seg = NSEG * D
        xg = fb[:, 0:seg].rearrange("p (c n) -> p c n", c=NSEG)
        xres = fb[:, seg:2 * seg].rearrange("p (c n) -> p c n", c=NSEG)
        xn2 = fb[:, 2 * seg:3 * seg].rearrange("p (c n) -> p c n", c=NSEG)
        yT_flat = fb[:, 3 * seg:]
        yT = yT_flat[:, 0:KD * HALF].rearrange("p (k n) -> p k n", k=KD)

        ident = sb("ident", [P, P], F32)
        tri = sb("tri", [P, P], BF16)
        ones_b = sb("ones_b", [P, P], BF16)
        mean_w = sb("mean_w", [P, P], F32)
        scal = sb("scal", [P, 5], F32)
        con = sb("con", [P, 16], F32)
        gate = sb("gate", [P, KD, E], F32)
        bn = sb("bn", [P, 4, 6], F32)
        mv = sb("mv", [P, 4, 2], F32)
        sd = sb("sd", [P, 4], F32)
        rs = sb("rs", [P, 4, 4], F32)
        aff = sb("aff", [P, 2, STEP_A, 4], F32)
        iota_i = sb("iota_i", [P, P], I32)
        iota_r = sb("iota_r", [P, P], F32)
        rev_i = sb("rev_i", [P, NT], I32)
        tok1 = sb("tok1", [P, NT], F32)
        lgs = sb("lgs", [P, NT, E], F32)
        ex = sb("ex", [P, NT, E], F32)
        key = sb("key", [P, NT, E], F32)
        mask = sb("mask", [P, NT, E], BF16)
        ex_key = sb("ex_key", [P, NT, E], F32)
        small = sb("small", [P, 12, NT], F32)
        cnt = sb("cnt", [P, 6, E], F32)
        over = sb("over", [P, MAX_OVER, E], F32)
        over2 = sb("over2", [P, MAX_OVER, E], F32)
        tab = sb("tab", [P, 4, NPT], F32)
        tab_i = sb("tab_i", [P, 4, NPT], I32)
        empty = sb("empty", [P, COLS], F32)
        slot_idx = sb("slot_idx", [P, COLS], I32)
        slot_p = sb("slot_p", [P, COLS], F32)
        idx_g = sb("idx_g", [P, NSEG], I32)
        idx_s = sb("idx_s", [P, NSEG], I32)
        p_g = sb("p_g", [P, NSEG], F32)
        p_s = sb("p_s", [P, NSEG], F32)

        row_acc = [psum("row_acc0"), psum("row_acc1")]
        y_acc = [psum(f"y_acc{k}") for k in range(KD)]
        tp = [psum("tp0"), psum("tp1")]
        logit_cols = y_acc[0][:, 0:(NT + 1) * E].rearrange("p (t e) -> p t e", t=NT + 1)
        logits = logit_cols[:, 1:NT + 1, :]
        prefix = y_acc[1][:, 0:NT * E]
        slots_ps = y_acc[2][:, 0:3 * COLS]
        counts_ps = y_acc[3][:, 0:E]
        stat_ps = y_acc[3][:, 16:18]

        inv_asf, k_x, k_w, k_sup, k_sq, k_out, eps_c, neg_magic, w_mean, w_scale = (
            con[:, i:i + 1] for i in range(10))

        small_in = sem("small_in")
        x_in_sem = [sem(f"x_in{g}") for g in range(4)]
        raw_in = [sem(f"raw_in{s}") for s in range(RING)]
        hi_ready = sem("hi_ready")
        lo_ready = sem("lo_ready")
        consts = sem("consts")
        chain_s = sem("vec_chain")
        achain_s = sem("act_chain")
        pool_s = sem("pool_chain")
        pool_tick = sem("pool_tick")
        vec_tick = sem("vec_tick")
        scal_ready = sem("scal_ready")
        w_stat_ready = sem("w_stat_ready")
        stat_mm = sem("stat_mm")
        wq_ready = sem("wq_ready")
        var_ready = sem("var_ready")
        sd_ready = sem("sd_ready")
        aff_ready = sem("aff_ready")
        xn_ready = sem("xn_ready")
        q_ready = sem("q_ready")
        tp_full = sem("tp_full")
        tp_free = sem("tp_free")
        qT_hi_ready = sem("qT_hi_ready")
        acc_full = sem("acc_full")
        sup_ready = sem("sup_ready")
        S_ready = sem("S_ready")
        x1_ready = sem("x1_ready")
        xn1_ready = sem("xn1_ready")
        xn1T_ready = sem("xn1T_ready")
        gate_done = sem("gate_done")
        rows_out = sem("rows_out")
        shift_ready = sem("shift_ready")
        exp_ready = sem("exp_ready")
        mask_ready = sem("mask_ready")
        pos_ready = sem("pos_ready")
        pay_ready = sem("pay_ready")
        slots_done = sem("slots_done")
        tab_ready = sem("tab_ready")
        staged = sem("staged")
        gathered = [sem(f"gathered{c}") for c in range(NSEG)]
        rows_kept = sem("rows_kept")
        ln_var = sem("ln_var")
        ln_sd = sem("ln_sd")
        xn2_ready = sem("xn2_ready")
        xt_full = sem("xt_full")
        xt_hi = sem("xt_hi")
        xt_lo = sem("xt_lo")
        h_full = sem("h_full")
        hh_ready = sem("hh_ready")
        hl_ready = sem("hl_ready")
        y_done = sem("y_done")
        yt_act = sem("yt_act")
        yt_vec = sem("yt_vec")
        fin_full = [sem(f"fin_full{c}") for c in range(NSEG)]
        rotated = sem("rotated")
        fin_ready = [sem(f"fin_ready{c}") for c in range(NSEG)]
        scattered = [sem(f"scattered{c}") for c in range(NSEG)]

        def piece(buf, slot, j):
            return buf[:, slot, j * PIECE:(j + 1) * PIECE]

        block = ctx.enter_context(nc.Block())

        @block.sync
        def _(sp):
            sp.dma_start(wraw, w_in).then_inc(small_in, 16)
            sp.dma_start(scal[:], scal_in).then_inc(small_in, 16)
            sp.dma_start(gate[:], gate_in).then_inc(small_in, 16)
            for g in range(4):
                sp.dma_start(x[:, 4 * g:4 * g + 4, :], x_in[:, 4 * g:4 * g + 4, :]).then_inc(x_in_sem[g], 16)
            for n in range(RING):
                sp.dma_start(raw[:, n, :], adj_in[n]).then_inc(raw_in[n], 16)
            with sp.Fori(1, NT // RING) as g:
                for s in range(RING):
                    sp.wait_ge(hi_ready, PIECES * (RING * g + s - RING + 1))
                    sp.wait_ge(lo_ready, PIECES * (RING * g + s - RING + 1))
                    sp.dma_start(raw[:, s, :], adj_in[bass.ds(RING * g + s, 1)].rearrange("a p n -> (a p) n")).then_inc(raw_in[s], 16)

            def load_pass(p, e):
                for i in range(2 * NC):
                    first = NT + 8 * p + i - RING + 1
                    sp.wait_ge(hi_ready, PIECES * first)
                    sp.wait_ge(lo_ready, PIECES * first)
                    sp.dma_start(raw[:, i % RING, :], experts_in[bass.ds(e * (2 * NC) + i, 1)].rearrange("a p n -> (a p) n")) \
                        .then_inc(raw_in[i % RING], 16)

            with sp.Fori(0, E) as p:
                load_pass(p, p)
            sp.wait_ge(tab_ready, 1)
            n_pass = sp.value_load(tab_i[0:1, 3, 0:1], min_val=E, max_val=E + MAX_OVER)
            with sp.If(n_pass > E):
                with sp.Fori(E, n_pass) as p:
                    e = sp.value_load(tab_i[0:1, 0, bass.ds(p, 1)], min_val=0, max_val=E - 1)
                    load_pass(p, e)

        @block.gpsimd
        def _(pool):
            ch = Chain(pool, pool_s)
            ch.done(nc.gpsimd.memset(ident[:], 0.0))
            ch.done(nc.gpsimd.memset(tri[:], 1.0))
            ch.done(nc.gpsimd.memset(ones_b[:], 1.0))
            ch.done(nc.gpsimd.memset(mean_w[:], 1.0 / P))
            ch.done(nc.gpsimd.iota(iota_i[:], pattern=[[1, P]], base=0, channel_multiplier=0))
            ch.done(nc.gpsimd.iota(rev_i[:], pattern=[[P, NT]], base=1, channel_multiplier=1))
            ch.wait()
            ch.done(nc.gpsimd.affine_select(out=ident[:], in_=ident[:], compare_op=ALU.not_equal, fill=1.0,
                                            base=0, pattern=[[-1, P]], channel_multiplier=1))
            ch.done(nc.gpsimd.affine_select(out=tri[:], in_=tri[:], compare_op=ALU.is_gt, fill=0.0,
                                            base=0, pattern=[[1, P]], channel_multiplier=-1))
            ch.done(nc.gpsimd.tensor_copy(iota_r[:], iota_i[:]))
            ch.done(nc.gpsimd.tensor_copy(tok1[:], rev_i[:]))
            ch.wait()
            pool.sem_inc(consts, 1)

            with pool.Fori(0, NT) as t:
                pool.wait_ge(x1_ready, t + 1)
                src = x[:, bass.ds(t, 1), :].rearrange("p a n -> p (a n)")
                pool.dma_start(x1_rows[bass.ds(t * P, P), :], src).then_inc(rows_out, 16)
                pool.dma_start(out[bass.ds(t * P, P), :], src).then_inc(rows_out, 16)

            pool.wait_ge(tab_ready, 1)
            pool.wait_ge(xn1T_ready, NT)
            ch.then(nc.gpsimd.memset(xg[:, 0:NSEG, :], 0.0))
            pool.wait_ge(rows_out, 32 * NT)
            n_pass = pool.value_load(tab_i[0:1, 3, 0:1], min_val=E, max_val=E + MAX_OVER)

            def gather(p):
                col = pool.value_load(tab_i[0:1, 1, bass.ds(p, 1)], min_val=0, max_val=COLS - NSEG)
                nc.gpsimd.tensor_copy(idx_g[:], slot_idx[:, bass.ds(col, NSEG)]).then_inc(staged, 1)
                nc.gpsimd.tensor_copy(p_g[:], slot_p[:, bass.ds(col, NSEG)]).then_inc(staged, 1)
                wait_apart(pool, staged, 2 * p + 2, pool_tick)
                for c, n in enumerate(SLOT_TILES):
                    nc.gpsimd.indirect_dma_start(
                        out=xg[0:n, c, :], out_offset=None, in_=x1_rows[:, :],
                        in_offset=bass.IndirectOffsetOnAxis(ap=idx_g[0:n, c:c + 1], axis=0),
                        bounds_check=T - 1, oob_is_err=False).then_inc(gathered[c], 16)

            def scatter(done):
                for c, n in enumerate(SLOT_TILES):
                    wait_apart(pool, fin_ready[c], done, pool_tick)
                    nc.gpsimd.indirect_dma_start(
                        out=out[:, :], out_offset=bass.IndirectOffsetOnAxis(ap=idx_s[0:n, c:c + 1], axis=0),
                        in_=xres[0:n, c, :], in_offset=None,
                        bounds_check=T - 1, oob_is_err=False).then_inc(scattered[c], 16)
                    wait_apart(pool, scattered[c], 16 * done, pool_tick)

            gather(0)
            with pool.Fori(0, n_pass) as p:
                with pool.If(p > 0):
                    scatter(p)
                nc.gpsimd.tensor_copy(idx_s[:], idx_g[:]).then_inc(rotated, 1)
                nc.gpsimd.tensor_copy(p_s[:], p_g[:]).then_inc(rotated, 1)
                wait_apart(pool, rotated, 2 * (p + 1), pool_tick)
                with pool.If(p + 1 < n_pass):
                    wait_apart(pool, rows_kept, NSEG * (p + 1), pool_tick)
                    gather(p + 1)
                    pool.nop()
            scatter(n_pass)

        @block.scalar
        def _(act):
            ch = Chain(act, achain_s)

            def split_hi(n_ready, slot, j, scale=None):
                if j == 0:
                    act.wait_ge(raw_in[slot], n_ready)
                nc.scalar.activation(piece(hi, slot, j), piece(raw, slot, j), ACT.Copy if scale is None else
                                     ACT.Identity, scale=1.0 if scale is None else scale).then_inc(hi_ready, 1)

            act.wait_ge(stat_mm, 2)
            act.wait_ge(scal_ready, 1)
            nc.scalar.activation(sd[:, 0:1], stat_ps[:, 1:2], ACT.Sqrt, scale=float(D * D) / (D * D - 1)) \
                .then_inc(sd_ready, 1)
            def row_stats(g):
                act.wait_ge(var_ready, g + 1)
                nc.scalar.activation(sd[:], mv[:, :, 1], ACT.Sqrt, bias=eps_c).then_inc(sd_ready, 1)

            for t in range(NT + 2):
                if t == 0:
                    row_stats(0)
                if t % STEP_A == 2 and t + 2 < NT:
                    row_stats((t + 2) // STEP_A)
                if t < NT:
                    g = t // STEP_A
                    act.wait_ge(aff_ready, g + 1)
                    if t >= 2:
                        act.wait_ge(tp_full, t - 1)
                    nc.scalar.activation(q[:, t % 2, :], x[:, t, :], ACT.Identity,
                                         scale=aff[:, g % 2, t % 4, 2:3], bias=aff[:, g % 2, t % 4, 3:4]) \
                        .then_inc(xn_ready, 1)
                if 1 <= t <= NT:
                    act.wait_ge(tp_full, t)
                    if t >= 3:
                        act.wait_ge(acc_full, t - 2)
                    nc.scalar.activation(qT_hi[:, (t - 1) % 2, :], tp[(t - 1) % 2][:], ACT.Identity,
                                         bias=neg_magic).then_inc(qT_hi_ready, 1)
                if t >= 2:
                    act.wait_ge(acc_full, t - 1)
                    if t >= 4:
                        act.wait_ge(S_ready, t - 3)
                    nc.scalar.activation(sup[:, t % 2, :], row_acc[t % 2][:], ACT.Relu, scale=k_sup) \
                        .then_inc(sup_ready, 1)
                if 3 <= t <= 5:
                    for j in range(PIECES):
                        split_hi(16, t - 3, j, inv_asf)

            def xn1T_copy(step, b):
                act.wait_ge(tp_full, NT + step)
                nc.scalar.activation(xn1T, tp[b][:].rearrange("p (k n) -> p k n", k=KD), ACT.Copy) \
                    .then_inc(xn1T_ready, 1)

            def group_b(g, last):
                for j in range(RING):
                    t = RING * g + j
                    slot = (j + 3) % RING
                    turn = g if j < 1 else g + 1
                    if not (last and j == 3):
                        act.wait_ge(acc_full, NT + t)
                        for i in range(PIECES):
                            split_hi(16 * (turn + 1), slot, i, None if last and j >= 1 else inv_asf)
                    if j == 0 and not last:
                        with act.If(g > 0):
                            xn1T_copy(t, 1)
                        with act.Else():
                            act.nop()
                    else:
                        xn1T_copy(t, (j - 1) % 2)
                    act.wait_ge(var_ready, NT // STEP_A + t + 1)
                    nc.scalar.activation(sd[:, 0:1], mv[:, 0, 1:2], ACT.Sqrt, bias=eps_c).then_inc(sd_ready, 1)

            with act.Fori(0, 3) as g:
                group_b(g, False)
            group_b(3, True)
            xn1T_copy(NT, 1)

            act.wait_ge(shift_ready, 1)
            nc.scalar.activation(ex[:], lgs[:], ACT.Exp).then_inc(exp_ready, 1)

            act.wait_ge(tab_ready, 1)
            n_pass = act.value_load(tab_i[0:1, 3, 0:1], min_val=E, max_val=E + MAX_OVER)

            def ln_rows(p):
                act.wait_ge(ln_var, p + 1)
                nc.scalar.activation(sd[:, 0:NSEG], mv[:, 0:NSEG, 1], ACT.Sqrt, bias=eps_c).then_inc(ln_sd, 1)

            def xT_copy(p, k):
                act.wait_ge(xt_full, KD * p + k + 1)
                nc.scalar.activation(xT_hi[:, k, :], tp[(k + 1) % 2][:, 0:HALF], ACT.Copy).then_inc(xt_hi, 1)

            ln_rows(0)
            for k in range(KD):
                xT_copy(0, k)
            with act.Fori(0, n_pass) as p:
                with act.If(p > 0):
                    act.wait_ge(y_done, NF * p)
                    for k in range(2):
                        nc.scalar.activation(yT[:, k, :], y_acc[k][:, 0:HALF], ACT.Copy).then_inc(yt_act, 1)
                with act.Else():
                    act.nop()
                for s in range(NF):
                    act.wait_ge(h_full, NF * p + s + 1)
                    if s >= 2:
                        act.wait_ge(y_done, NF * p + s - 1)
                    nc.scalar.activation(h_hi[:, s % 2, :], row_acc[s % 2][:, 0:HALF], ACT.Relu) \
                        .then_inc(hh_ready, 1)

                    def pieces():
                        item = 2 + s // 2
                        for j in ((0, 1) if s % 2 == 0 else (2, 3)):
                            split_hi(16 * (4 + 2 * p + item // RING + 1), item % RING, j)

                    if s < 3 * FC:
                        pieces()
                    else:
                        with act.If(p + 1 < n_pass):
                            if s == NF - 1:
                                for k in range(KD):
                                    xT_copy(p + 1, k)
                            pieces()
                        with act.Else():
                            act.nop()
                    if s == 7:
                        act.wait_ge(rotated, 2 * (p + 1))
                        for c in range(NSEG):
                            act.wait_ge(gathered[c], 16 * (p + 1))
                            nc.scalar.activation(xres[:, c, :], xg[:, c, :], ACT.Copy).then_inc(rows_kept, 1)
                    if s == 11:
                        with act.If(p + 1 < n_pass):
                            ln_rows(p + 1)
                        with act.Else():
                            act.nop()
                act.nop()
            act.wait_ge(y_done, NF * n_pass)
            for k in range(2):
                nc.scalar.activation(yT[:, k, :], y_acc[k][:, 0:HALF], ACT.Copy).then_inc(yt_act, 1)

        @block.vector
        def _(dve):
            ch = Chain(dve, chain_s)
            v = nc.vector

            def split_lo(done, slot, j, scale=None):
                dve.wait_ge(hi_ready, done + j + 1)
                a, b = piece(raw, slot, j), piece(hi, slot, j).bitcast(F32)
                if scale is None:
                    v.tensor_tensor(piece(lo, slot, j), a, b, ALU.subtract).then_inc(lo_ready, 1)
                else:
                    v.scalar_tensor_tensor(out=piece(lo, slot, j), in0=a, scalar=scale, in1=b, op0=ALU.mult,
                                           op1=ALU.subtract).then_inc(lo_ready, 1)

            def rsqrt(r, var, n, dev):
                ch.done(v.reciprocal(r[:, 0:n, 0], dev[:, 0:n]))
                ch.then(v.tensor_scalar(r[:, 0:n, 1], var, EPS, None, ALU.add))
                ch.then(v.tensor_tensor(r[:, 0:n, 1], r[:, 0:n, 1], r[:, 0:n, 0], ALU.mult))
                ch.then(v.tensor_tensor(r[:, 0:n, 1], r[:, 0:n, 1], r[:, 0:n, 0], ALU.mult))
                ch.then(v.tensor_scalar(r[:, 0:n, 1], r[:, 0:n, 1], -0.5, 1.5, ALU.mult, ALU.add))
                ch.then(v.tensor_tensor(r[:, 0:n, 0], r[:, 0:n, 0], r[:, 0:n, 1], ALU.mult))

            dve.sem_inc(tp_free, 2)
            for bank in (*y_acc, *row_acc, *tp):
                ch.done(v.memset(bank[:], 0.0))
            ch.done(v.memset(yT_flat[:, KD * HALF:], 0.0))
            ch.done(v.memset(rs[:], 0.0))
            ch.done(v.memset(mv[:], 0.0))
            ch.done(v.memset(tab[:], 0.0))
            ch.done(v.memset(eps_c, EPS))
            ch.done(v.memset(neg_magic, -MAGIC))
            dve.wait_ge(small_in, 48)
            asf, a_w, a_x, a_2 = (scal[:, i:i + 1] for i in range(4))
            ch.done(v.reciprocal(inv_asf, asf))
            ch.done(v.reciprocal(k_x, a_x))
            ch.done(v.reciprocal(k_w, a_w))
            ch.done(v.reciprocal(k_sq, a_2))
            ch.done(v.tensor_scalar(k_sup, a_x, a_w, 1.0 / (ACT_N * WGT_N), ALU.mult, ALU.mult))
            ch.then(v.tensor_scalar(k_out, asf, a_2, 1.0 / ACT_N, ALU.mult, ALU.mult))
            ch.done(v.tensor_scalar(k_x, k_x, ACT_N, None, ALU.mult))
            ch.done(v.tensor_scalar(k_w, k_w, WGT_N, None, ALU.mult))
            ch.then(v.tensor_scalar(k_sq, k_sq, ACT_N, None, ALU.mult))
            dve.sem_inc(scal_ready, 1)
            for k in range(KD):
                ch.done(v.bn_stats(bn[:, k, :], wraw[:, k, :]))
            ch.wait()
            ch.then(v.bn_aggr(mv[:, 0, :], bn[:].rearrange("p a b -> p (a b)")))
            dve.sem_inc(w_stat_ready, 1)
            dve.wait_ge(stat_mm, 1)
            ch.then(v.tensor_copy(w_mean, stat_ps[:, 0:1]))
            ch.then(v.tensor_scalar(rs[:, 0, 0:1], mv[:, 0, 0:1], w_mean, None, ALU.subtract))
            ch.then(v.tensor_tensor(rs[:, 0, 0:1], rs[:, 0, 0:1], rs[:, 0, 0:1], ALU.mult))
            ch.then(v.tensor_tensor(mv[:, 1, 0:1], rs[:, 0, 0:1], mv[:, 0, 1:2], ALU.add))
            dve.sem_inc(w_stat_ready, 1)
            dve.wait_ge(sd_ready, 1)
            ch.then(v.reciprocal(w_scale, sd[:, 0:1]))
            ch.then(v.tensor_tensor(w_scale, w_scale, k_w, ALU.mult))
            ch.then(v.tensor_scalar(wraw, wraw, w_mean, w_scale, ALU.subtract, ALU.mult))
            ch.then(v.tensor_scalar(wraw, wraw, WGT_N, -WGT_N, ALU.min, ALU.max))
            v.tensor_scalar(wq, wraw, MAGIC, MAGIC, ALU.add, ALU.subtract).then_inc(wq_ready, 1)

            def row_stats(g):
                dve.wait_ge(x_in_sem[g], 16)
                for j in range(STEP_A):
                    ch.done(v.bn_stats(bn[:, j, :], x[:, STEP_A * g + j, :]))
                ch.wait()
                for j in range(STEP_A):
                    last = v.bn_aggr(mv[:, j, :], bn[:, j, :])
                    if j < STEP_A - 1:
                        ch.done(last)
                last.then_inc(var_ready, 1)
                dve.wait_ge(var_ready, g + 1)
                dve.wait_ge(sd_ready, g + 2)
                a = aff[:, g % 2]
                rsqrt(a, mv[:, :, 1], STEP_A, sd)
                ch.then(v.tensor_scalar(a[:, :, 2], a[:, :, 0], k_x, None, ALU.mult))
                v.scalar_tensor_tensor(out=a[:, :, 3], in0=mv[:, :, 0], scalar=-1.0, in1=a[:, :, 2],
                                       op0=ALU.mult, op1=ALU.mult).then_inc(aff_ready, 1)

            for t in range(NT + 3):
                if t == 0:
                    row_stats(0)
                if t % STEP_A == 2 and t + 2 < NT:
                    row_stats((t + 2) // STEP_A)
                if t < NT:
                    dve.wait_ge(xn_ready, t + 1)
                    v.tensor_scalar(q[:, t % 2, :], q[:, t % 2, :], ACT_N, MAGIC, ALU.min, ALU.add) \
                        .then_inc(q_ready, 1)
                if 1 <= t <= NT:
                    dve.wait_ge(qT_hi_ready, t)
                    v.scalar_tensor_tensor(out=qT_lo[:, (t - 1) % 2, :], in0=tp[(t - 1) % 2][:], scalar=-MAGIC,
                                           in1=qT_hi[:, (t - 1) % 2, :].bitcast(F32), op0=ALU.add,
                                           op1=ALU.subtract).then_inc(tp_free, 1)
                if t >= 3:
                    u = t - 3
                    dve.wait_ge(sup_ready, u + 1)
                    ch.then(v.tensor_scalar(sup[:, u % 2, :], sup[:, u % 2, :], k_sq, ACT_N, ALU.mult, ALU.min))
                    v.tensor_scalar(S[:, u, :], sup[:, u % 2, :], MAGIC, MAGIC, ALU.add, ALU.subtract) \
                        .then_inc(S_ready, 1)
                if 3 <= t <= 5:
                    for j in range(PIECES):
                        split_lo(PIECES * (t - 3), t - 3, j, inv_asf)

            def group_b(g, last):
                for j in range(4):
                    t = 4 * g + j
                    slot = (j + 3) % RING
                    if not (last and j == 3):
                        for i in range(PIECES):
                            split_lo(PIECES * (t + 3), slot, i, None if last and j >= 1 else inv_asf)
                    dve.wait_ge(acc_full, NT + t + 1)
                    xt = x[:, bass.ds(t, 1), :].rearrange("p a n -> p (a n)")
                    v.scalar_tensor_tensor(out=xt, in0=row_acc[j % 2][:], scalar=k_out, in1=xt, op0=ALU.mult,
                                           op1=ALU.add).then_inc(x1_ready, 1)
                    wait_apart(dve, x1_ready, t + 1, vec_tick)
                    ch.done(v.bn_stats(bn[:, 0, :], xt))
                    wait_apart(dve, chain_s, ch.base + ch.n, vec_tick)
                    v.bn_aggr(mv[:, 0, :], bn[:, 0, :]).then_inc(var_ready, 1)
                    dve.wait_ge(var_ready, 4 + t + 1)
                    dve.wait_ge(sd_ready, 5 + t + 1)
                    rsqrt(rs, mv[:, 0:1, 1], 1, sd)
                    dve.wait_ge(tp_full, NT + t)
                    v.tensor_scalar(xn1, xt, mv[:, 0, 0:1], rs[:, 0, 0:1], ALU.subtract, ALU.mult) \
                        .then_inc(xn1_ready, 1)

            per_group = 4 * 7
            start = ch.n
            with dve.Fori(0, 3) as g:
                ch.base, ch.n = g * per_group, start
                group_b(g, False)
                assert ch.n == start + per_group, (ch.n - start)
            ch.base, ch.n = 0, start + 3 * per_group
            group_b(3, True)

            dve.wait_ge(consts, 1)
            dve.wait_ge(gate_done, NT)

            def sm(i):
                return small[:, i, :]

            def over_e(a, n=E):
                return a.unsqueeze(2).to_broadcast([P, NT, n])

            mx, km, tot, prob, pos, half, pp, cf, rr, kc, big, p_hi = (sm(i) for i in range(12))
            ch.then(v.tensor_reduce(mx, logits, AX, ALU.max))
            v.tensor_tensor(lgs[:], logits, over_e(mx), ALU.subtract).then_inc(shift_ready, 1)
            dve.wait_ge(shift_ready, 1)
            rev = iota_r[:, 0:E].unsqueeze(1).to_broadcast([P, NT, E])
            ch.then(v.tensor_scalar(key[:], lgs[:], 0.0, float(E), ALU.is_equal, ALU.mult))
            ch.then(v.scalar_tensor_tensor(out=ex_key[:], in0=lgs[:], scalar=0.0, in1=rev, op0=ALU.is_equal,
                                           op1=ALU.mult))
            ch.then(v.tensor_tensor(key[:], key[:], ex_key[:], ALU.subtract))
            ch.then(v.tensor_reduce(km, key[:], AX, ALU.max))
            v.tensor_tensor(mask[:], key[:], over_e(km), ALU.is_equal).then_inc(mask_ready, 1)
            dve.wait_ge(exp_ready, 1)
            ch.then(v.tensor_reduce(tot, ex[:], AX, ALU.add))
            ch.then(v.reciprocal(prob, tot))
            dve.wait_ge(pos_ready, 1)
            dve.wait_ge(mask_ready, 1)
            ch.then(v.tensor_tensor(key[:], prefix.rearrange("p (t e) -> p t e", t=NT), mask[:], ALU.mult))
            ch.then(v.tensor_reduce(pos, key[:], AX, ALU.add))
            ch.done(v.tensor_scalar(big, pos, float(CAP), 1000.0, ALU.is_ge, ALU.mult))
            ch.then(v.tensor_scalar(half, pos, float(HALF), None, ALU.is_ge))
            ch.then(v.scalar_tensor_tensor(out=pp, in0=half, scalar=-float(HALF), in1=pos, op0=ALU.mult, op1=ALU.add))
            ch.then(v.tensor_scalar(cf, pp, -(P - 1) / 2.0, 1.0 / P, ALU.add, ALU.mult))
            ch.then(v.tensor_scalar(cf, cf, MAGIC, MAGIC, ALU.add, ALU.subtract))
            ch.done(v.scalar_tensor_tensor(out=rr, in0=cf, scalar=-float(P), in1=pp, op0=ALU.mult, op1=ALU.add))
            ch.then(v.scalar_tensor_tensor(out=kc, in0=km, scalar=-2.0 * NSEG, in1=cf, op0=ALU.mult, op1=ALU.add))
            ch.then(v.scalar_tensor_tensor(out=kc, in0=half, scalar=float(NSEG), in1=kc, op0=ALU.mult, op1=ALU.add))
            ch.then(v.scalar_tensor_tensor(out=kc, in0=kc, scalar=float(COLS), in1=big, op0=ALU.add, op1=ALU.add))
            ch.done(v.tensor_tensor(r_hot, iota_r[:].unsqueeze(1).to_broadcast([P, NT, P]), over_e(rr, P),
                                    ALU.is_equal))
            ch.then(v.tensor_tensor(col_hot, iota_r[:, 0:COLS].unsqueeze(1).to_broadcast([P, NT, COLS]),
                                    over_e(kc, COLS), ALU.is_equal))
            ch.done(v.tensor_tensor(payload[:, :, 0, :], col_hot, over_e(tok1[:], COLS), ALU.mult))
            ch.then(v.tensor_tensor(payload[:, :, 1, :], col_hot, over_e(prob, COLS), ALU.mult))
            ch.then(v.tensor_tensor(col_hot, col_hot, over_e(prob, COLS), ALU.mult))
            v.tensor_tensor(payload[:, :, 2, :], col_hot, payload[:, :, 1, :].bitcast(F32), ALU.subtract) \
                .then_inc(pay_ready, 1)
            ov, incl, tmp = cnt[:, 1, :], cnt[:, 2, :], cnt[:, 3, :]
            ch.then(v.tensor_copy(cnt[:, 0, :], counts_ps))
            ch.done(v.tensor_copy(tab[:, 2, 0:E], cnt[:, 0, :]))
            ch.done(v.tensor_copy(tab[:, 0, 0:E], iota_r[:, 0:E]))
            ch.done(v.tensor_scalar(tab[:, 1, 0:E], iota_r[:, 0:E], 2.0 * NSEG, None, ALU.mult))
            ch.done(v.tensor_scalar(ov, cnt[:, 0, :], float(HALF), None, ALU.is_gt))
            ch.then(v.tensor_scalar(incl, cnt[:, 0, :], float(HALF), None, ALU.is_gt))
            for sh in (1, 2, 4):
                ch.then(v.tensor_copy(tmp, incl))
                ch.then(v.tensor_tensor(incl[:, sh:E], tmp[:, sh:E], tmp[:, 0:E - sh], ALU.add))
            ch.then(v.tensor_tensor(tmp, incl, ov, ALU.mult))
            ch.then(v.tensor_tensor(over[:], tmp.unsqueeze(1).to_broadcast([P, MAX_OVER, E]),
                                    iota_r[:, 1:1 + MAX_OVER].unsqueeze(2).to_broadcast([P, MAX_OVER, E]),
                                    ALU.is_equal))
            ch.then(v.tensor_tensor(over2[:], over[:], iota_r[:, 0:E].unsqueeze(1).to_broadcast([P, MAX_OVER, E]),
                                    ALU.mult))
            ch.then(v.tensor_reduce(tab[:, 0, E:E + MAX_OVER], over2[:], AX, ALU.add))
            ch.then(v.tensor_tensor(over2[:], over[:], cnt[:, 0, :].unsqueeze(1).to_broadcast([P, MAX_OVER, E]),
                                    ALU.mult))
            ch.then(v.tensor_reduce(tab[:, 2, E:E + MAX_OVER], over2[:], AX, ALU.add))
            ch.done(v.tensor_scalar(tab[:, 2, E:E + MAX_OVER], tab[:, 2, E:E + MAX_OVER], -float(HALF), None,
                                    ALU.add))
            ch.done(v.tensor_scalar(tab[:, 1, E:E + MAX_OVER], tab[:, 0, E:E + MAX_OVER], 2.0 * NSEG, float(NSEG),
                                    ALU.mult, ALU.add))
            ch.then(v.tensor_scalar(tab[:, 3, 0:1], incl[:, E - 1:E], float(E), None, ALU.add))
            ch.then(v.tensor_copy(tab_i[:], tab[:]))
            dve.wait_ge(slots_done, 1)
            ch.done(v.tensor_scalar(empty[:], slots_ps[:, 0:COLS], 0.0, 2.0 * T, ALU.is_equal, ALU.mult))
            ch.then(v.tensor_copy(slot_p[:], slots_ps[:, COLS:2 * COLS]))
            ch.done(v.tensor_tensor(slot_p[:], slots_ps[:, 2 * COLS:3 * COLS], slot_p[:], ALU.add))
            ch.then(v.scalar_tensor_tensor(out=slot_idx[:], in0=slots_ps[:, 0:COLS], scalar=-1.0, in1=empty[:],
                                           op0=ALU.add, op1=ALU.add))
            dve.sem_inc(tab_ready, 1)

            n_pass = dve.value_load(tab_i[0:1, 3, 0:1], min_val=E, max_val=E + MAX_OVER)

            def ln_stats(p, c):
                n = SLOT_TILES[c]
                wait_apart(dve, gathered[c], 16 * (p + 1), vec_tick)
                ch.done(v.bn_stats(bn[0:n, c, :], xg[0:n, c, :]))

            def ln_var_out():
                wait_apart(dve, chain_s, ch.base + ch.n, vec_tick)
                for c, n in enumerate(SLOT_TILES):
                    ch.done(v.bn_aggr(mv[0:n, c, :], bn[0:n, c, :]))
                ch.wait()
                dve.sem_inc(ln_var, 1)

            def ln_scale(p):
                dve.wait_ge(ln_sd, p + 1)
                rsqrt(rs, mv[:, 0:NSEG, 1], NSEG, sd)

            def ln_out(cs):
                for c in cs:
                    n = SLOT_TILES[c]
                    v.tensor_scalar(xn2[0:n, c, :], xg[0:n, c, :], mv[0:n, c, 0:1], rs[0:n, c, 0:1],
                                    ALU.subtract, ALU.mult).then_inc(xn2_ready, 1)

            LN_CHAIN = 2 * NSEG + 6

            def xT_copy(p, k):
                dve.wait_ge(xt_hi, KD * p + k + 1)
                v.tensor_tensor(xT_lo[:, k, :], tp[(k + 1) % 2][:, 0:HALF], xT_hi[:, k, :].bitcast(F32),
                                ALU.subtract).then_inc(xt_lo, 1)

            def y_copy(p):
                dve.wait_ge(y_done, NF * p)
                for k in range(2, KD):
                    v.tensor_copy(yT[:, k, :], y_acc[k][:, 0:HALF]).then_inc(yt_vec, 1)

            def final(done, cs):
                for c in cs:
                    n = SLOT_TILES[c]
                    dve.wait_ge(fin_full[c], done)
                    dve.wait_ge(rows_kept, NSEG * done)
                    v.scalar_tensor_tensor(out=xres[0:n, c, :], in0=tp[c % 2][0:n, :], scalar=p_s[0:n, c:c + 1],
                                           in1=xres[0:n, c, :], op0=ALU.mult, op1=ALU.add).then_inc(fin_ready[c], 1)

            for c in range(NSEG):
                ln_stats(0, c)
            ln_var_out()
            ln_scale(0)
            ln_out(range(NSEG))
            for k in range(KD):
                xT_copy(0, k)
            start = ch.n
            with dve.Fori(0, n_pass) as p:
                ch.base, ch.n = p * LN_CHAIN, start
                with dve.If(p > 0):
                    y_copy(p)
                with dve.Else():
                    dve.nop()
                for s in range(NF):
                    dve.wait_ge(hh_ready, NF * p + s + 1)
                    v.scalar_tensor_tensor(out=h_lo[:, s % 2, :], in0=row_acc[s % 2][:, 0:HALF], scalar=0.0,
                                           in1=h_hi[:, s % 2, :].bitcast(F32), op0=ALU.max,
                                           op1=ALU.subtract).then_inc(hl_ready, 1)

                    def pieces():
                        item = 2 + s // 2
                        for j in ((0, 1) if s % 2 == 0 else (2, 3)):
                            split_lo(PIECES * (NT + 8 * p + item), item % RING, j)

                    if s in (1, 2):
                        with dve.If(p > 0):
                            final(p, (0, 1) if s == 1 else (2,))
                        with dve.Else():
                            dve.nop()
                    if s < 10:
                        pieces()
                        continue
                    if s < 3 * FC:
                        pieces()
                    with dve.If(p + 1 < n_pass):
                        if s == NF - 1:
                            for k in range(KD):
                                xT_copy(p + 1, k)
                        if s >= 3 * FC:
                            pieces()
                        if s == 10:
                            ln_stats(p + 1, 0)
                            ln_stats(p + 1, 1)
                        if s == 11:
                            ln_stats(p + 1, 2)
                            ln_var_out()
                        if s == 12:
                            ln_scale(p + 1)
                            ln_out([0])
                        if s == 13:
                            ln_out([1, 2])
                    with dve.Else():
                        dve.nop()
                dve.nop()
            y_copy(n_pass)
            final(n_pass, range(NSEG))

        @block.tensor
        def _(pe):
            mm = nc.tensor.matmul
            pe.wait_ge(consts, 1)
            for i in range(2):
                pe.wait_ge(w_stat_ready, i + 1)
                src = mv[:, 0, 0:1] if i == 0 else mv[:, 1, 0:1]
                mm(stat_ps[:, i:i + 1], mean_w[:], src, start=True, stop=True).then_inc(stat_mm, 1)
            for t in range(NT + 1):
                if t < NT:
                    pe.wait_ge(q_ready, t + 1)
                    pe.wait_ge(tp_free, t + 1)
                    for k in range(KD):
                        last = nc.tensor.transpose(tp[t % 2][:, k * P:(k + 1) * P],
                                                   q[:, t % 2, k * P:(k + 1) * P], ident[:])
                    last.then_inc(tp_full, 1)
                if t == 1:
                    pe.wait_ge(wq_ready, 1)
                if t >= 1:
                    u = t - 1
                    pe.wait_ge(tp_free, 2 + u + 1)
                    if u >= 2:
                        pe.wait_ge(sup_ready, u - 1)
                    for k in range(KD):
                        for part in (qT_hi, qT_lo):
                            last = mm(row_acc[u % 2][:], part[:, u % 2, k * P:(k + 1) * P], wq[:, k, :],
                                      start=(k == 0 and part is qT_hi), stop=(k == KD - 1 and part is qT_lo))
                    last.then_inc(acc_full, 1)

            def gate_in(step, b):
                pe.wait_ge(xn1_ready, step)
                for k in range(KD):
                    last = nc.tensor.transpose(tp[b][:, k * P:(k + 1) * P], xn1[:, k * P:(k + 1) * P], ident[:])
                last.then_inc(tp_full, 1)

            def gate_out(step):
                pe.wait_ge(xn1T_ready, step)
                dst = logit_cols[:, bass.ds(step, 1), :].rearrange("p a e -> p (a e)")
                for k in range(KD):
                    last = mm(dst, xn1T[:, k, :], gate[:, k, :], start=(k == 0), stop=(k == KD - 1))
                last.then_inc(gate_done, 1)

            def adj_rows(t, j, jts, stop):
                for jt in jts:
                    for part in (hi, lo):
                        last = mm(row_acc[j % 2][:], part[:, j, jt * P:(jt + 1) * P], S[:, jt, :],
                                  start=(jt == 0 and part is hi), stop=(jt == NT - 1 and part is lo))
                if stop:
                    last.then_inc(acc_full, 1)

            def group_b(g, last):
                for j in range(4):
                    t = 4 * g + j
                    pe.wait_ge(lo_ready, PIECES * (t + 1))
                    adj_rows(t, j, range(10), False)
                    if j == 0 and not last:
                        with pe.If(g > 0):
                            gate_in(t, 1)
                        with pe.Else():
                            pe.nop()
                    else:
                        gate_in(t, (j - 1) % 2)
                    adj_rows(t, j, range(10, NT), True)
                    if j == 0 and not last:
                        with pe.If(g > 0):
                            gate_out(t)
                        with pe.Else():
                            pe.nop()
                    else:
                        gate_out(t)

            pe.wait_ge(S_ready, NT)
            with pe.Fori(0, 3) as g:
                group_b(g, False)
            group_b(3, True)
            gate_in(NT, 1)
            gate_out(NT)

            pe.wait_ge(mask_ready, 1)
            mflat = mask[:].rearrange("p t e -> p (t e)")
            mm(prefix, tri[:], mflat, start=True, stop=False)
            for sh in range(1, NT):
                last = mm(prefix[:, sh * E:NT * E], ones_b[:], mflat[:, 0:(NT - sh) * E], start=False,
                          stop=(sh == NT - 1))
            for t in range(NT):
                last = mm(counts_ps, ones_b[:], mask[:, t, :], start=(t == 0), stop=(t == NT - 1))
            last.then_inc(pos_ready, 1)
            pe.wait_ge(pay_ready, 1)
            for t in range(NT):
                last = mm(slots_ps, r_hot[:, t, :], payload[:, t, :, :].rearrange("p j c -> p (j c)"),
                          start=(t == 0), stop=(t == NT - 1))
            last.then_inc(slots_done, 1)

            pe.wait_ge(tab_ready, 1)
            n_pass = pe.value_load(tab_i[0:1, 3, 0:1], min_val=E, max_val=E + MAX_OVER)

            def xT(p, k):
                pe.wait_ge(xn2_ready, NSEG * (p + 1))
                if k >= 2:
                    pe.wait_ge(xt_lo, KD * p + k - 1)
                at = 0
                for c, n in enumerate(SLOT_TILES):
                    last = nc.tensor.transpose(tp[(k + 1) % 2][:, at:at + n], xn2[0:n, c, k * P:(k + 1) * P],
                                               ident[0:n, 0:n])
                    at += n
                last.then_inc(xt_full, 1)

            def final(done, c):
                if c == 0:
                    pe.wait_ge(yt_act, 2 * done)
                    pe.wait_ge(yt_vec, 2 * done)
                if c >= 2:
                    pe.wait_ge(fin_ready[c - 2], done)
                for k in range(KD):
                    at = k * HALF + c * P
                    last = nc.tensor.transpose(tp[c % 2][:, k * P:(k + 1) * P], yT_flat[:, at:at + P], ident[:])
                last.then_inc(fin_full[c], 1)

            def up(p, s, w):
                item = 2 * (s // FC)
                if s % FC == 0:
                    pe.wait_ge(lo_ready, PIECES * (NT + 8 * p + item + 1))
                if s >= 2:
                    pe.wait_ge(hl_ready, NF * p + s - 1)
                for k in range(KD):
                    if s == 0:
                        pe.wait_ge(xt_lo, KD * p + k + 1)
                    at = k * FC * P + (s % FC) * P
                    for i, (a, b) in enumerate(((hi, xT_hi), (hi, xT_lo), (lo, xT_hi))):
                        last = mm(row_acc[s % 2][:, 0:w], a[:, item % RING, at:at + P], b[:, k, 0:w],
                                  start=(k == 0 and i == 0), stop=(k == KD - 1 and i == 2))
                last.then_inc(h_full, 1)

            def down(p, s, w):
                item = 2 * (s // FC) + 1
                if s % FC == 0:
                    pe.wait_ge(lo_ready, PIECES * (NT + 8 * p + item + 1))
                pe.wait_ge(hl_ready, NF * p + s + 1)
                for k in range(KD):
                    at = (s % FC) * D + k * P
                    for i, (a, b) in enumerate(((hi, h_hi), (hi, h_lo), (lo, h_hi))):
                        last = mm(y_acc[k][:, 0:w], a[:, item % RING, at:at + P], b[:, s % 2, 0:w],
                                  start=(s == 0 and i == 0), stop=(s == NF - 1 and i == 2))
                last.then_inc(y_done, 1)

            def expert_pass(p, w):
                for s in range(NF):
                    if s == NF - 1:
                        with pe.If(p + 1 < n_pass):
                            pe.wait_ge(rotated, 2 * (p + 1))
                            xT(p + 1, 0)
                            xT(p + 1, 1)
                        with pe.Else():
                            pe.nop()
                    up(p, s, w)
                    if s == 1:
                        with pe.If(p > 0):
                            final(p, 0)
                            final(p, 1)
                        with pe.Else():
                            pe.nop()
                    if s >= 1:
                        down(p, s - 1, w)
                    if s == 1:
                        with pe.If(p > 0):
                            final(p, 2)
                        with pe.Else():
                            pe.nop()
                with pe.If(p + 1 < n_pass):
                    xT(p + 1, 2)
                    xT(p + 1, 3)
                with pe.Else():
                    pe.nop()
                down(p, NF - 1, w)

            for k in range(KD):
                xT(0, k)
            with pe.Fori(0, n_pass) as p:
                n_tok = pe.value_load(tab_i[0:1, 2, bass.ds(p, 1)])
                with pe.If(n_tok <= WIDTHS[0]):
                    expert_pass(p, WIDTHS[0])
                with pe.Else():
                    with pe.If(n_tok <= WIDTHS[1]):
                        expert_pass(p, WIDTHS[1])
                    with pe.Else():
                        expert_pass(p, WIDTHS[2])
                    pe.nop()
                pe.nop()
            for c in range(NSEG):
                final(n_pass, c)


def kernel(**inputs):
    import numpy as np
    import concourse.bacc as bacc
    from concourse import mybir as mb
    from concourse.bass_utils import run_bass_kernel_spmd

    f = {k: np.asarray(a) for k, a in inputs.items()}
    arrays = {
        "x_rows": f["x"].reshape(NT, P, D).transpose(1, 0, 2),
        "adj_tiles": f["adj"].reshape(NT, P, NT, P).transpose(0, 3, 2, 1).reshape(NT, P, ITEM),
        "gnn_weight": f["L0_gnn_weight"].reshape(KD, P, D).transpose(1, 0, 2),
        "scales": np.broadcast_to(np.stack([f["L0_gnn_" + k].reshape(()) for k in (
            "adj_scaling_factor", "wgt_alpha", "act_alpha", "act_alpha2", "act_alpha2")]), (P, 5)),
        "gate_w": f["L0_ffn_gate_w"].reshape(KD, P, E).transpose(1, 0, 2),
        "experts": np.stack([
            f["L0_ffn_w1"].reshape(E, KD, P, NC, FC * P).transpose(0, 3, 2, 1, 4).reshape(E, NC, P, ITEM),
            f["L0_ffn_w2"].reshape(E, NC, FC, P, D).transpose(0, 1, 3, 2, 4).reshape(E, NC, P, ITEM),
        ], axis=2).reshape(E * NC * 2, P, ITEM),
    }
    arrays = {k: np.ascontiguousarray(a) for k, a in arrays.items()}
    nc = bacc.Bacc("TRN2", target_bir_lowering=False, num_devices=1)
    ins = [nc.dram_tensor(k, a.shape, mb.dt.from_np(a.dtype), kind="ExternalInput").ap()
           for k, a in arrays.items()]
    out = nc.dram_tensor("out_rows", (T, D), mb.dt.float32, kind="ExternalOutput").ap()
    x1_rows = nc.dram_tensor("x1_rows", (T, D), mb.dt.float32, kind="Internal").ap()
    gnn_moe_kernel(nc, ins[0], ins[1], ins[2], ins[3], ins[4], ins[5], out, x1_rows)
    r = run_bass_kernel_spmd(nc, [arrays], core_ids=[0])
    return r.results[0]["out_rows"]
```

```python
from contextlib import ExitStack

import concourse.bass as bass
from concourse import mybir

P = 128
T, D, E, F, CAP = 2048, 512, 8, 2048, 640
NT = T // P
KD = D // P
NF = F // P
FC = 4
NC = NF // FC
HALF = CAP // 2
SLOT_TILES = [P, P, HALF - 2 * P]
NSEG = len(SLOT_TILES)
MAX_OVER = T // (HALF + 1)
NPT = E + MAX_OVER + 2
COLS = E * 2 * NSEG
WIDTHS = list(range(256, HALF, 16)) + [HALF]
ITEM = NT * P
RING = 4
PIECES = 4
PIECE = ITEM // PIECES
MAGIC = 12582912.0
EPS = 1e-5
ACT_N = 15.0
WGT_N = 7.0
STEP_A = 4
CODE_MAX = 4095.0
KEEP_AT = [5, 6, 8]

ALU = mybir.AluOpType
ACT = mybir.ActivationFunctionType
AX = mybir.AxisListType.X
F32 = mybir.dt.float32
F32R = mybir.dt.float32r
BF16 = mybir.dt.bfloat16
I32 = mybir.dt.int32


class Chain:

    def __init__(self, engine, sem):
        self.engine, self.sem, self.n, self.base = engine, sem, 0, 0

    def done(self, ins):
        ins.then_inc(self.sem, 1)
        self.n += 1

    def wait(self):
        self.engine.wait_ge(self.sem, self.base + self.n)

    def then(self, ins):
        self.done(ins)
        self.wait()


def wait_apart(engine, sem, value, tick):
    engine.wait_ge(sem, value)
    engine.sem_inc(tick, 1)


def gnn_moe_kernel(nc, x_in, adj_in, w_in, scal_in, gate_in, experts_in, out, x1_rows):
    with ExitStack() as ctx:
        def sb(name, shape, dt):
            return ctx.enter_context(nc.sbuf_tensor(name, shape, dt))

        def psum(name):
            return ctx.enter_context(nc.psum_tensor(name, [P, 512], F32))

        def sem(name):
            return ctx.enter_context(nc.semaphore(name))

        raw = sb("raw", [P, RING, ITEM], F32)
        hi = sb("hi", [P, RING, ITEM], F32R)
        lo = sb("lo", [P, RING, ITEM], F32R)
        x = sb("x", [P, NT, D], F32)
        S = sb("S", [P, NT, D], F32R)
        fr = sb("fr", [P, 8 * 512], F32R)
        fb = sb("fb", [P, 3 * NSEG * D + KD * HALF + P - SLOT_TILES[-1]], F32)

        wq = fr[:, 0:KD * D].rearrange("p (k n) -> p k n", k=KD)
        qT_hi = fr[:, 2048:3072].rearrange("p (b n) -> p b n", b=2)
        qT_lo = fr[:, 3072:4096].rearrange("p (b n) -> p b n", b=2)
        wraw = fb[:, 0:KD * D].rearrange("p (k n) -> p k n", k=KD)
        q = fb[:, 2048:3072].rearrange("p (b n) -> p b n", b=2)
        sup = fb[:, 3072:4096].rearrange("p (b n) -> p b n", b=2)
        xn1 = fb[:, 4096:4608]
        xn1T = fb[:, 4608:5120].rearrange("p (k n) -> p k n", k=KD)
        r_hot = S[:, 0:4, :].rearrange("p a b -> p (a b)").rearrange("p (t r) -> p t r", t=NT)
        payload = S[:, 4:9, :].rearrange("p a b -> p (a b)")[:, 0:NT * 3 * COLS] \
            .rearrange("p (t j c) -> p t j c", t=NT, j=3)
        col_hot = fb[:, 2048:2048 + NT * COLS].rearrange("p (t c) -> p t c", t=NT)
        xT_hi = fr[:, 0:KD * HALF].rearrange("p (k n) -> p k n", k=KD)
        xT_lo = fr[:, KD * HALF:2 * KD * HALF].rearrange("p (k n) -> p k n", k=KD)
        h_hi = fr[:, 8 * HALF:10 * HALF].rearrange("p (b n) -> p b n", b=2)
        h_lo = fr[:, 10 * HALF:12 * HALF].rearrange("p (b n) -> p b n", b=2)
        seg = NSEG * D
        xg = fb[:, 0:seg].rearrange("p (c n) -> p c n", c=NSEG)
        xres = fb[:, seg:2 * seg].rearrange("p (c n) -> p c n", c=NSEG)
        xn2 = fb[:, 2 * seg:3 * seg].rearrange("p (c n) -> p c n", c=NSEG)
        yT_flat = fb[:, 3 * seg:]
        yT = yT_flat[:, 0:KD * HALF].rearrange("p (k n) -> p k n", k=KD)

        ident = sb("ident", [P, P], F32)
        tri = sb("tri", [P, P], BF16)
        ones_b = sb("ones_b", [P, P], BF16)
        mean_w = sb("mean_w", [P, P], F32)
        scal = sb("scal", [P, 5], F32)
        con = sb("con", [P, 16], F32)
        gate = sb("gate", [P, KD, E], F32)
        bn = sb("bn", [P, 4, 6], F32)
        mv = sb("mv", [P, 4, 2], F32)
        sd = sb("sd", [P, 4], F32)
        bn_w = sb("bn_w", [P, KD, 6], F32)
        mv_w = sb("mv_w", [P, 2, 2], F32)
        w_dev = sb("w_dev", [P, 1], F32)
        w_off = sb("w_off", [P, 1], F32)
        need_f = sb("need_f", [P, 1], F32)
        need_lo = sb("need_lo", [P, 1], I32)
        rs = sb("rs", [P, 4, 4], F32)
        aff = sb("aff", [P, 2, STEP_A, 4], F32)
        iota_i = sb("iota_i", [P, P], I32)
        iota_r = sb("iota_r", [P, P], F32)
        rev_i = sb("rev_i", [P, NT], I32)
        tok1 = sb("tok1", [P, NT], F32)
        lgs = sb("lgs", [P, NT, E], F32)
        ex = sb("ex", [P, NT, E], F32)
        key = sb("key", [P, NT, E], F32)
        mask = sb("mask", [P, NT, E], BF16)
        rev_e = sb("rev_e", [P, E], F32)
        small = sb("small", [P, 11, NT], F32)
        cnt = sb("cnt", [P, 6, E], F32)
        over = sb("over", [P, MAX_OVER, E], F32)
        over2 = sb("over2", [P, MAX_OVER, E], F32)
        tab = sb("tab", [P, 4, NPT], F32)
        tab_i = sb("tab_i", [P, 4, NPT], I32)
        empty = sb("empty", [P, COLS], F32)
        slot_idx = sb("slot_idx", [P, COLS], I32)
        slot_p = sb("slot_p", [P, COLS], F32)
        idx_g = sb("idx_g", [P, NSEG], I32)
        idx_s = sb("idx_s", [P, NSEG], I32)
        p_g = sb("p_g", [P, NSEG], F32)
        p_s = sb("p_s", [P, NSEG], F32)

        row_acc = [psum("row_acc0"), psum("row_acc1")]
        y_acc = [psum(f"y_acc{k}") for k in range(KD)]
        tp = [psum("tp0"), psum("tp1")]
        logit_cols = y_acc[0][:, 0:(NT + 1) * E].rearrange("p (t e) -> p t e", t=NT + 1)
        logits = logit_cols[:, 1:NT + 1, :]
        prefix = y_acc[1][:, 0:NT * E]
        tok_ps = y_acc[2][:, 0:COLS]
        prob_ps = row_acc[0][:, 0:2 * COLS]
        counts_ps = y_acc[3][:, 0:E]
        stat_ps = y_acc[3][:, 16:18]

        inv_asf, k_x, k_w, k_sup, k_sq, k_out, eps_c, neg_magic, w_mean, w_scale = (
            con[:, i:i + 1] for i in range(10))

        small_in = sem("small_in")
        w_in_sem = sem("w_in_sem")
        x_in_sem = [sem(f"x_in{g}") for g in range(4)]
        raw_in = [sem(f"raw_in{s}") for s in range(RING)]
        hi_ready = sem("hi_ready")
        lo_ready = sem("lo_ready")
        consts = sem("consts")
        chain_s = sem("vec_chain")
        achain_s = sem("act_chain")
        pool_s = sem("pool_chain")
        pool_tick = sem("pool_tick")
        vec_tick = sem("vec_tick")
        scal_ready = sem("scal_ready")
        need_ready = sem("need_ready")
        w_stat_ready = sem("w_stat_ready")
        stat_mm = sem("stat_mm")
        wq_ready = sem("wq_ready")
        var_ready = sem("var_ready")
        sd_ready = sem("sd_ready")
        aff_ready = sem("aff_ready")
        xn_ready = sem("xn_ready")
        q_ready = sem("q_ready")
        tp_full = sem("tp_full")
        tp_free = sem("tp_free")
        qT_hi_ready = sem("qT_hi_ready")
        acc_full = sem("acc_full")
        sup_ready = sem("sup_ready")
        S_ready = sem("S_ready")
        x1_ready = sem("x1_ready")
        xn1_ready = sem("xn1_ready")
        xn1T_ready = sem("xn1T_ready")
        gate_done = sem("gate_done")
        rows_out = sem("rows_out")
        shift_ready = sem("shift_ready")
        exp_ready = sem("exp_ready")
        mask_ready = sem("mask_ready")
        pos_ready = sem("pos_ready")
        tok_ready = sem("tok_ready")
        prob_ready = sem("prob_ready")
        r_hot_ready = sem("r_hot_ready")
        tok_done = sem("tok_done")
        idx_ready = sem("idx_ready")
        counts_done = sem("counts_done")
        prob_done = sem("prob_done")
        tab_ready = sem("tab_ready")
        staged = sem("staged")
        gathered = [sem(f"gathered{c}") for c in range(NSEG)]
        rows_kept = sem("rows_kept")
        ln_var = sem("ln_var")
        ln_sd = sem("ln_sd")
        ln_aff = sem("ln_aff")
        xn2_ready = sem("xn2_ready")
        xt_full = sem("xt_full")
        xt_hi = sem("xt_hi")
        xt_lo = sem("xt_lo")
        h_full = sem("h_full")
        hh_ready = sem("hh_ready")
        hl_ready = sem("hl_ready")
        y_done = sem("y_done")
        yt_act = sem("yt_act")
        yt_vec = sem("yt_vec")
        fin_full = [sem(f"fin_full{c}") for c in range(NSEG)]
        rotated = sem("rotated")
        fin_ready = [sem(f"fin_ready{c}") for c in range(NSEG)]
        scattered = [sem(f"scattered{c}") for c in range(NSEG)]

        def piece(buf, slot, j):
            return buf[:, slot, j * PIECE:(j + 1) * PIECE]

        def first_items(t):
            k = t - STEP_A
            return [(k // PIECES, k % PIECES)] if 0 <= k < (RING - 1) * PIECES else []

        def ring_work(s):
            if s < 3 * FC:
                return [(2 + s // 2, (0, 1) if s % 2 == 0 else (2, 3))]
            return {12: [(8, (0, 1, 2))], 13: [(8, (3,)), (9, (0,))], 14: [(9, (1, 2))], 15: [(9, (3,))]}[s]

        block = ctx.enter_context(nc.Block())

        @block.sync
        def _(sp):
            sp.dma_start(scal[:], scal_in).then_inc(small_in, 16)
            sp.dma_start(gate[:], gate_in).then_inc(small_in, 16)
            for g in range(4):
                sp.dma_start(x[:, 4 * g:4 * g + 4, :], x_in[:, 4 * g:4 * g + 4, :]).then_inc(x_in_sem[g], 16)
                if g == 0:
                    sp.dma_start(wraw, w_in).then_inc(w_in_sem, 16)
            for n in range(RING):
                sp.dma_start(raw[:, n, :], adj_in[n]).then_inc(raw_in[n], 16)
            with sp.Fori(1, NT // RING) as g:
                for s in range(RING):
                    sp.wait_ge(hi_ready, PIECES * (RING * g + s - RING + 1))
                    sp.wait_ge(lo_ready, PIECES * (RING * g + s - RING + 1))
                    sp.dma_start(raw[:, s, :], adj_in[bass.ds(RING * g + s, 1)].rearrange("a p n -> (a p) n")).then_inc(raw_in[s], 16)

            def load_pass(p, e):
                for i in range(2 * NC):
                    first = NT + 8 * p + i - RING + 1
                    sp.wait_ge(hi_ready, PIECES * first)
                    sp.wait_ge(lo_ready, PIECES * first)
                    sp.dma_start(raw[:, i % RING, :], experts_in[bass.ds(e * (2 * NC) + i, 1)].rearrange("a p n -> (a p) n")) \
                        .then_inc(raw_in[i % RING], 16)

            with sp.Fori(0, E) as p:
                load_pass(p, p)
            sp.wait_ge(tab_ready, 1)
            n_pass = sp.value_load(tab_i[0:1, 3, 0:1], min_val=E, max_val=E + MAX_OVER)
            with sp.If(n_pass > E):
                with sp.Fori(E, n_pass) as p:
                    e = sp.value_load(tab_i[0:1, 0, bass.ds(p, 1)], min_val=0, max_val=E - 1)
                    load_pass(p, e)

        @block.gpsimd
        def _(pool):
            ch = Chain(pool, pool_s)
            ch.done(nc.gpsimd.memset(ident[:], 0.0))
            ch.done(nc.gpsimd.memset(tri[:], 1.0))
            ch.done(nc.gpsimd.memset(ones_b[:], 1.0))
            ch.done(nc.gpsimd.memset(mean_w[:], 1.0 / P))
            ch.done(nc.gpsimd.iota(iota_i[:], pattern=[[1, P]], base=0, channel_multiplier=0))
            ch.done(nc.gpsimd.iota(rev_i[:], pattern=[[P, NT]], base=1, channel_multiplier=1))
            ch.wait()
            ch.done(nc.gpsimd.affine_select(out=ident[:], in_=ident[:], compare_op=ALU.not_equal, fill=1.0,
                                            base=0, pattern=[[-1, P]], channel_multiplier=1))
            ch.done(nc.gpsimd.affine_select(out=tri[:], in_=tri[:], compare_op=ALU.is_gt, fill=0.0,
                                            base=0, pattern=[[1, P]], channel_multiplier=-1))
            ch.done(nc.gpsimd.tensor_copy(iota_r[:], iota_i[:]))
            ch.done(nc.gpsimd.tensor_copy(tok1[:], rev_i[:]))
            ch.wait()
            pool.sem_inc(consts, 1)
            pool.wait_ge(wq_ready, 1)
            ch.then(nc.gpsimd.memset(xg[:, 0:NSEG, :], 0.0))

            def gather_dma(c, n):
                nc.gpsimd.indirect_dma_start(
                    out=xg[0:n, c, :], out_offset=None, in_=x1_rows[:, :],
                    in_offset=bass.IndirectOffsetOnAxis(ap=idx_g[0:n, c:c + 1], axis=0),
                    bounds_check=T - 1, oob_is_err=False).then_inc(gathered[c], 16)

            with pool.Fori(0, NT) as t:
                pool.wait_ge(x1_ready, t + 1)
                src = x[:, bass.ds(t, 1), :].rearrange("p a n -> p (a n)")
                pool.dma_start(x1_rows[bass.ds(t * P, P), :], src).then_inc(rows_out, 16)
                pool.dma_start(out[bass.ds(t * P, P), :], src).then_inc(rows_out, 16)

            pool.wait_ge(rows_out, 32 * NT)
            pool.wait_ge(idx_ready, 1)
            nc.gpsimd.tensor_copy(idx_g[:], slot_idx[:, 0:NSEG]).then_inc(staged, NSEG)
            pool.wait_ge(staged, NSEG)
            for c, n in enumerate(SLOT_TILES):
                gather_dma(c, n)
            pool.wait_ge(tab_ready, 1)
            nc.gpsimd.tensor_copy(p_g[:], slot_p[:, 0:NSEG]).then_inc(staged, NSEG)
            pool.wait_ge(staged, 2 * NSEG)
            n_pass = pool.value_load(tab_i[0:1, 3, 0:1], min_val=E, max_val=E + MAX_OVER)

            def gather(p, c):
                n = SLOT_TILES[c]
                col = pool.value_load(tab_i[0:1, 1, bass.ds(p, 1)], min_val=0, max_val=COLS - NSEG)
                nc.gpsimd.tensor_copy(idx_g[:, c:c + 1], slot_idx[:, bass.ds(col + c, 1)]).then_inc(staged, 1)
                nc.gpsimd.tensor_copy(p_g[:, c:c + 1], slot_p[:, bass.ds(col + c, 1)]).then_inc(staged, 1)
                wait_apart(pool, staged, 2 * NSEG * p + 2 * (c + 1), pool_tick)
                gather_dma(c, n)

            def scatter(done, c):
                n = SLOT_TILES[c]
                wait_apart(pool, fin_ready[c], done, pool_tick)
                nc.gpsimd.indirect_dma_start(
                    out=out[:, :], out_offset=bass.IndirectOffsetOnAxis(ap=idx_s[0:n, c:c + 1], axis=0),
                    in_=xres[0:n, c, :], in_offset=None,
                    bounds_check=T - 1, oob_is_err=False).then_inc(scattered[c], 16)

            def rotate(p, c):
                nc.gpsimd.tensor_copy(idx_s[:, c:c + 1], idx_g[:, c:c + 1]).then_inc(rotated, 1)
                nc.gpsimd.tensor_copy(p_s[:, c:c + 1], p_g[:, c:c + 1]).then_inc(rotated, 1)
                wait_apart(pool, rotated, 2 * NSEG * p + 2 * (c + 1), pool_tick)

            def gather_next(p, c):
                with pool.If(p + 1 < n_pass):
                    wait_apart(pool, rows_kept, NSEG * p + c + 1, pool_tick)
                    gather(p + 1, c)
                    pool.nop()

            with pool.Fori(0, n_pass) as p:
                for c in range(NSEG):
                    with pool.If(p > 0):
                        scatter(p, c)
                        pool.nop()
                    if c >= 1:
                        gather_next(p, c - 1)
                    with pool.If(p > 0):
                        wait_apart(pool, scattered[c], 16 * p, pool_tick)
                    rotate(p, c)
                gather_next(p, NSEG - 1)
            for c in range(NSEG):
                scatter(n_pass, c)
                wait_apart(pool, scattered[c], 16 * n_pass, pool_tick)

        @block.scalar
        def _(act):
            ch = Chain(act, achain_s)

            def split_hi(n_ready, slot, j, scale=None):
                if j == 0:
                    act.wait_ge(raw_in[slot], n_ready)
                nc.scalar.activation(piece(hi, slot, j), piece(raw, slot, j), ACT.Copy if scale is None else
                                     ACT.Identity, scale=1.0 if scale is None else scale).then_inc(hi_ready, 1)

            def row_stats(g):
                act.wait_ge(var_ready, g + 1)
                nc.scalar.activation(sd[:], mv[:, :, 1], ACT.Sqrt, bias=eps_c).then_inc(sd_ready, 1)

            row_stats(0)
            act.wait_ge(stat_mm, 2)
            act.wait_ge(scal_ready, 1)
            nc.scalar.activation(w_dev[:], stat_ps[:, 1:2], ACT.Sqrt, scale=float(D * D) / (D * D - 1)) \
                .then_inc(sd_ready, 1)
            for t in range(NT + 2):
                if t < NT:
                    g = t // STEP_A
                    act.wait_ge(aff_ready, g + 1)
                    if t >= 2:
                        act.wait_ge(tp_full, t - 1)
                    nc.scalar.activation(q[:, t % 2, :], x[:, t, :], ACT.Identity,
                                         scale=aff[:, g % 2, t % 4, 2:3], bias=aff[:, g % 2, t % 4, 3:4]) \
                        .then_inc(xn_ready, 1)
                if 1 <= t <= NT:
                    act.wait_ge(tp_full, t)
                    if t >= 3:
                        act.wait_ge(acc_full, t - 2)
                    nc.scalar.activation(qT_hi[:, (t - 1) % 2, :], tp[(t - 1) % 2][:], ACT.Identity,
                                         bias=neg_magic).then_inc(qT_hi_ready, 1)
                if t >= 2:
                    act.wait_ge(acc_full, t - 1)
                    if t >= 4:
                        act.wait_ge(S_ready, t - 3)
                    nc.scalar.activation(sup[:, t % 2, :], row_acc[t % 2][:], ACT.Relu, scale=k_sup) \
                        .then_inc(sup_ready, 1)
                for item, j in first_items(t):
                    split_hi(16, item, j, inv_asf)
                if t % STEP_A == 2 and t + 2 < NT:
                    row_stats((t + 2) // STEP_A)

            def xn1T_copy(step, b):
                act.wait_ge(tp_full, NT + step)
                nc.scalar.activation(xn1T, tp[b][:].rearrange("p (k n) -> p k n", k=KD), ACT.Copy) \
                    .then_inc(xn1T_ready, 1)

            def group_b(g, last):
                for j in range(RING):
                    t = RING * g + j
                    slot = (j + 3) % RING
                    turn = g if j < 1 else g + 1
                    if not (last and j == 3):
                        act.wait_ge(acc_full, NT + t)
                        for i in range(PIECES):
                            split_hi(16 * (turn + 1), slot, i, None if last and j >= 1 else inv_asf)
                    if j == 0 and not last:
                        with act.If(g > 0):
                            xn1T_copy(t, 1)
                        with act.Else():
                            act.nop()
                    else:
                        xn1T_copy(t, (j - 1) % 2)
                    act.wait_ge(var_ready, NT // STEP_A + t + 1)
                    nc.scalar.activation(sd[:, 0:1], mv[:, 0, 1:2], ACT.Sqrt, bias=eps_c).then_inc(sd_ready, 1)

            with act.Fori(0, 3) as g:
                group_b(g, False)
            group_b(3, True)
            xn1T_copy(NT, 1)

            act.wait_ge(shift_ready, 1)
            nc.scalar.activation(ex[:], lgs[:], ACT.Exp).then_inc(exp_ready, 1)


            def ln_rows(p):
                act.wait_ge(ln_var, p + 1)
                nc.scalar.activation(sd[:, 0:NSEG], mv[:, 0:NSEG, 1], ACT.Sqrt, bias=eps_c).then_inc(ln_sd, 1)

            def xT_copy(p, k):
                act.wait_ge(xt_full, KD * p + k + 1)
                nc.scalar.activation(xT_hi[:, k, :], tp[(k + 1) % 2][:, 0:HALF], ACT.Copy).then_inc(xt_hi, 1)

            def ln_out(p, cs):
                for c in cs:
                    n = SLOT_TILES[c]
                    act.wait_ge(ln_aff, p + 1)
                    nc.scalar.activation(xn2[0:n, c, :], xg[0:n, c, :], ACT.Identity, scale=rs[0:n, c, 0:1],
                                         bias=rs[0:n, c, 3:4]).then_inc(xn2_ready, 1)

            ln_rows(0)
            ln_out(0, range(NSEG))
            for k in range(KD):
                xT_copy(0, k)
            act.wait_ge(tab_ready, 1)
            n_pass = act.value_load(tab_i[0:1, 3, 0:1], min_val=E, max_val=E + MAX_OVER)
            with act.Fori(0, n_pass) as p:
                with act.If(p > 0):
                    act.wait_ge(y_done, NF * p)
                    for k in range(2):
                        nc.scalar.activation(yT[:, k, :], y_acc[k][:, 0:HALF], ACT.Copy).then_inc(yt_act, 1)
                with act.Else():
                    act.nop()
                for s in range(NF):
                    act.wait_ge(h_full, NF * p + s + 1)
                    if s >= 2:
                        act.wait_ge(y_done, NF * p + s - 1)
                    nc.scalar.activation(h_hi[:, s % 2, :], row_acc[s % 2][:, 0:HALF], ACT.Relu) \
                        .then_inc(hh_ready, 1)

                    def pieces():
                        for item, js in ring_work(s):
                            for j in js:
                                split_hi(16 * (4 + 2 * p + item // RING + 1), item % RING, j)

                    if s < 3 * FC:
                        pieces()
                    else:
                        with act.If(p + 1 < n_pass):
                            if s == NF - 1:
                                xT_copy(p + 1, 0)
                                xT_copy(p + 1, 1)
                            if s in (13, 14):
                                ln_out(p + 1, (0, 1) if s == 13 else (2,))
                            pieces()
                            if s == NF - 1:
                                xT_copy(p + 1, 2)
                                xT_copy(p + 1, 3)
                        with act.Else():
                            act.nop()
                    if s == 11:
                        with act.If(p + 1 < n_pass):
                            ln_rows(p + 1)
                        with act.Else():
                            act.nop()
                    if s in KEEP_AT:
                        c = KEEP_AT.index(s)
                        act.wait_ge(rotated, 2 * NSEG * p + 2 * (c + 1))
                        act.wait_ge(gathered[c], 16 * (p + 1))
                        nc.scalar.activation(xres[:, c, :], xg[:, c, :], ACT.Copy).then_inc(rows_kept, 1)
                act.nop()
            act.wait_ge(y_done, NF * n_pass)
            for k in range(2):
                nc.scalar.activation(yT[:, k, :], y_acc[k][:, 0:HALF], ACT.Copy).then_inc(yt_act, 1)

        @block.vector
        def _(dve):
            ch = Chain(dve, chain_s)
            v = nc.vector

            def split_lo(done, slot, j, scale=None):
                dve.wait_ge(hi_ready, done + j + 1)
                a, b = piece(raw, slot, j), piece(hi, slot, j).bitcast(F32)
                if scale is None:
                    v.tensor_tensor(piece(lo, slot, j), a, b, ALU.subtract).then_inc(lo_ready, 1)
                else:
                    v.scalar_tensor_tensor(out=piece(lo, slot, j), in0=a, scalar=scale, in1=b, op0=ALU.mult,
                                           op1=ALU.subtract).then_inc(lo_ready, 1)

            def rsqrt(r, var, n, dev):
                root, tmp = r[:, 0:n, 0], r[:, 0:n, 1]
                ch.then(v.reciprocal(root, dev[:, 0:n]))
                ch.then(v.scalar_tensor_tensor(out=tmp, in0=var, scalar=EPS, in1=root, op0=ALU.add, op1=ALU.mult))
                ch.then(v.scalar_tensor_tensor(out=tmp, in0=tmp, scalar=-0.5, in1=root, op0=ALU.mult, op1=ALU.mult))
                ch.then(v.scalar_tensor_tensor(out=root, in0=tmp, scalar=1.5, in1=root, op0=ALU.add, op1=ALU.mult))

            dve.sem_inc(tp_free, 2)
            for bank in (*y_acc, *row_acc, *tp):
                ch.done(v.memset(bank[:], 0.0))
            ch.done(v.memset(yT_flat[:, KD * HALF:], 0.0))
            ch.done(v.memset(rs[:], 0.0))
            ch.done(v.memset(mv[:], 0.0))
            ch.done(v.memset(tab[:], 0.0))
            ch.done(v.memset(eps_c, EPS))
            ch.done(v.memset(neg_magic, -MAGIC))
            dve.wait_ge(small_in, 32)
            asf, a_w, a_x, a_2 = (scal[:, i:i + 1] for i in range(4))
            ch.done(v.reciprocal(inv_asf, asf))
            ch.done(v.reciprocal(k_x, a_x))
            ch.done(v.reciprocal(k_w, a_w))
            ch.done(v.reciprocal(k_sq, a_2))
            ch.done(v.tensor_scalar(k_sup, a_x, a_w, 1.0 / (ACT_N * WGT_N), ALU.mult, ALU.mult))
            ch.then(v.tensor_scalar(k_out, asf, a_2, 1.0 / ACT_N, ALU.mult, ALU.mult))
            ch.done(v.tensor_scalar(k_x, k_x, ACT_N, None, ALU.mult))
            ch.done(v.tensor_scalar(k_w, k_w, WGT_N, None, ALU.mult))
            ch.then(v.tensor_scalar(k_sq, k_sq, ACT_N, None, ALU.mult))
            dve.sem_inc(scal_ready, 1)
            ch.then(v.tensor_tensor(need_f[:], k_x, k_x, ALU.mult))
            ch.then(v.tensor_scalar(need_f[:], need_f[:], CODE_MAX * CODE_MAX / D, None, ALU.is_gt))
            v.tensor_copy(need_lo[:], need_f[:]).then_inc(need_ready, 1)
            dve.wait_ge(need_ready, 1)
            need = dve.value_load(need_lo[0:1, 0:1], min_val=0, max_val=1)
            def tile_stats(t):
                g, j = t // STEP_A, t % STEP_A
                if j == 0:
                    dve.wait_ge(x_in_sem[g], 16)
                ch.done(v.bn_stats(bn[:, j, :], x[:, t, :]))
                if j == STEP_A - 1:
                    ch.wait()
                    for i in range(STEP_A):
                        last = v.bn_aggr(mv[:, i, :], bn[:, i, :])
                        if i < STEP_A - 1:
                            ch.done(last)
                    last.then_inc(var_ready, 1)

            def row_scales(g):
                dve.wait_ge(var_ready, g + 1)
                ch.wait()
                dve.wait_ge(sd_ready, g + 2 if g else 1)
                a = aff[:, g % 2]
                rsqrt(a, mv[:, :, 1], STEP_A, sd)
                ch.then(v.tensor_scalar(a[:, :, 2], a[:, :, 0], k_x, None, ALU.mult))
                v.scalar_tensor_tensor(out=a[:, :, 3], in0=mv[:, :, 0], scalar=-1.0, in1=a[:, :, 2],
                                       op0=ALU.mult, op1=ALU.mult).then_inc(aff_ready, 1)

            for j in range(STEP_A):
                tile_stats(j)
            dve.wait_ge(w_in_sem, 16)
            for k in range(KD):
                ch.done(v.bn_stats(bn_w[:, k, :], wraw[:, k, :]))
            ch.wait()
            ch.then(v.bn_aggr(mv_w[:, 0, :], bn_w[:].rearrange("p a b -> p (a b)")))
            dve.sem_inc(w_stat_ready, 1)
            row_scales(0)
            dve.wait_ge(stat_mm, 1)
            ch.then(v.tensor_copy(w_mean, stat_ps[:, 0:1]))
            ch.then(v.tensor_scalar(w_off[:], mv_w[:, 0, 0:1], w_mean, None, ALU.subtract))
            ch.then(v.tensor_tensor(w_off[:], w_off[:], w_off[:], ALU.mult))
            ch.then(v.tensor_tensor(mv_w[:, 1, 0:1], w_off[:], mv_w[:, 0, 1:2], ALU.add))
            dve.sem_inc(w_stat_ready, 1)
            dve.wait_ge(sd_ready, 2)
            ch.then(v.reciprocal(w_scale, w_dev[:]))
            ch.then(v.tensor_tensor(w_scale, w_scale, k_w, ALU.mult))
            ch.then(v.tensor_scalar(wraw, wraw, w_mean, w_scale, ALU.subtract, ALU.mult))
            ch.then(v.tensor_scalar(wraw, wraw, WGT_N, -WGT_N, ALU.min, ALU.max))
            v.tensor_scalar(wq, wraw, MAGIC, MAGIC, ALU.add, ALU.subtract).then_inc(wq_ready, 1)

            for t in range(NT + 3):
                if t < NT:
                    dve.wait_ge(xn_ready, t + 1)
                    v.tensor_scalar(q[:, t % 2, :], q[:, t % 2, :], ACT_N, MAGIC, ALU.min, ALU.add) \
                        .then_inc(q_ready, 1)
                if 1 <= t <= NT:
                    dve.wait_ge(qT_hi_ready, t)
                    with dve.If(need > 0):
                        v.scalar_tensor_tensor(out=qT_lo[:, (t - 1) % 2, :], in0=tp[(t - 1) % 2][:], scalar=-MAGIC,
                                               in1=qT_hi[:, (t - 1) % 2, :].bitcast(F32), op0=ALU.add,
                                               op1=ALU.subtract).then_inc(tp_free, 1)
                    with dve.Else():
                        dve.sem_inc(tp_free, 1)
                if t >= 3:
                    u = t - 3
                    dve.wait_ge(sup_ready, u + 1)
                    ch.then(v.tensor_scalar(sup[:, u % 2, :], sup[:, u % 2, :], k_sq, ACT_N, ALU.mult, ALU.min))
                    v.tensor_scalar(S[:, u, :], sup[:, u % 2, :], MAGIC, MAGIC, ALU.add, ALU.subtract) \
                        .then_inc(S_ready, 1)
                nxt = STEP_A * (t // STEP_A + 1)
                if nxt < NT:
                    for j in ((0, 1), (2,), (3,), ())[t % STEP_A]:
                        tile_stats(nxt + j)
                    if t % STEP_A == STEP_A - 1:
                        row_scales(nxt // STEP_A)
                for item, j in first_items(t):
                    split_lo(PIECES * item, item, j, inv_asf)

            def group_b(g, last):
                for j in range(4):
                    t = 4 * g + j
                    slot = (j + 3) % RING
                    if not (last and j == 3):
                        for i in range(PIECES):
                            split_lo(PIECES * (t + 3), slot, i, None if last and j >= 1 else inv_asf)
                    dve.wait_ge(acc_full, NT + t + 1)
                    xt = x[:, bass.ds(t, 1), :].rearrange("p a n -> p (a n)")
                    v.scalar_tensor_tensor(out=xt, in0=row_acc[j % 2][:], scalar=k_out, in1=xt, op0=ALU.mult,
                                           op1=ALU.add).then_inc(x1_ready, 1)
                    wait_apart(dve, x1_ready, t + 1, vec_tick)
                    ch.done(v.bn_stats(bn[:, 0, :], xt))
                    wait_apart(dve, chain_s, ch.base + ch.n, vec_tick)
                    v.bn_aggr(mv[:, 0, :], bn[:, 0, :]).then_inc(var_ready, 1)
                    dve.wait_ge(var_ready, 4 + t + 1)
                    dve.wait_ge(sd_ready, 5 + t + 1)
                    rsqrt(rs, mv[:, 0:1, 1], 1, sd)
                    dve.wait_ge(tp_full, NT + t)
                    v.tensor_scalar(xn1, xt, mv[:, 0, 0:1], rs[:, 0, 0:1], ALU.subtract, ALU.mult) \
                        .then_inc(xn1_ready, 1)

            per_group = 4 * 5
            start = ch.n
            with dve.Fori(0, 3) as g:
                ch.base, ch.n = g * per_group, start
                group_b(g, False)
                assert ch.n == start + per_group, (ch.n - start)
            ch.base, ch.n = 0, start + 3 * per_group
            group_b(3, True)

            dve.wait_ge(consts, 1)
            ch.then(v.tensor_scalar(rev_e[:], iota_r[:, 0:E], -1.0, float(E), ALU.mult, ALU.add))
            dve.wait_ge(gate_done, NT)

            def sm(i):
                return small[:, i, :]

            def over_e(a, n=E):
                return a.unsqueeze(2).to_broadcast([P, NT, n])

            mx, km, tot, prob, pos, half, pp, cf, rr, kc, big = (sm(i) for i in range(11))
            ch.then(v.tensor_reduce(mx, logits, AX, ALU.max))
            v.tensor_tensor(lgs[:], logits, over_e(mx), ALU.subtract).then_inc(shift_ready, 1)
            dve.wait_ge(shift_ready, 1)
            ch.then(v.scalar_tensor_tensor(out=key[:], in0=lgs[:], scalar=0.0,
                                           in1=rev_e[:].unsqueeze(1).to_broadcast([P, NT, E]),
                                           op0=ALU.is_equal, op1=ALU.mult))
            ch.then(v.tensor_reduce(km, key[:], AX, ALU.max))
            v.tensor_tensor(mask[:], key[:], over_e(km), ALU.is_equal).then_inc(mask_ready, 1)
            dve.wait_ge(pos_ready, 1)
            dve.wait_ge(mask_ready, 1)
            ch.then(v.tensor_tensor(key[:], prefix.rearrange("p (t e) -> p t e", t=NT), mask[:], ALU.mult))
            ch.then(v.tensor_reduce(pos, key[:], AX, ALU.add))
            ch.done(v.tensor_scalar(big, pos, float(CAP), 1000.0, ALU.is_ge, ALU.mult))
            ch.then(v.tensor_scalar(half, pos, float(HALF), None, ALU.is_ge))
            ch.then(v.scalar_tensor_tensor(out=pp, in0=half, scalar=-float(HALF), in1=pos, op0=ALU.mult, op1=ALU.add))
            ch.then(v.tensor_scalar(cf, pp, -(P - 1) / 2.0, 1.0 / P, ALU.add, ALU.mult))
            ch.then(v.tensor_scalar(cf, cf, MAGIC, MAGIC, ALU.add, ALU.subtract))
            ch.done(v.scalar_tensor_tensor(out=rr, in0=cf, scalar=-float(P), in1=pp, op0=ALU.mult, op1=ALU.add))
            ch.then(v.scalar_tensor_tensor(out=kc, in0=km, scalar=-2.0 * NSEG, in1=cf, op0=ALU.mult, op1=ALU.add))
            ch.then(v.scalar_tensor_tensor(out=kc, in0=half, scalar=float(NSEG), in1=kc, op0=ALU.mult, op1=ALU.add))
            ch.then(v.scalar_tensor_tensor(out=kc, in0=kc, scalar=float(COLS), in1=big, op0=ALU.add, op1=ALU.add))
            ch.then(v.tensor_tensor(col_hot, iota_r[:, 0:COLS].unsqueeze(1).to_broadcast([P, NT, COLS]),
                                    over_e(kc, COLS), ALU.is_equal))
            v.tensor_tensor(payload[:, :, 0, :], col_hot, over_e(tok1[:], COLS), ALU.mult).then_inc(tok_ready, 1)
            for ts in (slice(0, NT // 2), slice(NT // 2, NT)):
                v.tensor_tensor(r_hot[:, ts, :], iota_r[:].unsqueeze(1).to_broadcast([P, NT // 2, P]),
                                rr[:, ts].unsqueeze(2).to_broadcast([P, NT // 2, P]), ALU.is_equal) \
                    .then_inc(r_hot_ready, 1)
            dve.wait_ge(exp_ready, 1)
            ch.then(v.tensor_reduce(tot, ex[:], AX, ALU.add))
            ch.then(v.reciprocal(prob, tot))
            dve.wait_ge(tok_ready, 1)
            ch.then(v.tensor_tensor(payload[:, :, 1, :], col_hot, over_e(prob, COLS), ALU.mult))
            ov, incl, tmp = cnt[:, 1, :], cnt[:, 2, :], cnt[:, 3, :]
            dve.wait_ge(counts_done, 1)
            ch.then(v.tensor_copy(cnt[:, 0, :], counts_ps))
            ch.done(v.tensor_copy(tab[:, 2, 0:E], cnt[:, 0, :]))
            ch.done(v.tensor_copy(tab[:, 0, 0:E], iota_r[:, 0:E]))
            ch.done(v.tensor_scalar(tab[:, 1, 0:E], iota_r[:, 0:E], 2.0 * NSEG, None, ALU.mult))
            ch.done(v.tensor_scalar(ov, cnt[:, 0, :], float(HALF), None, ALU.is_gt))
            ch.then(v.tensor_scalar(incl, cnt[:, 0, :], float(HALF), None, ALU.is_gt))
            for sh in (1, 2, 4):
                ch.then(v.tensor_copy(tmp, incl))
                ch.then(v.tensor_tensor(incl[:, sh:E], tmp[:, sh:E], tmp[:, 0:E - sh], ALU.add))
            ch.then(v.tensor_tensor(tmp, incl, ov, ALU.mult))
            dve.wait_ge(tok_done, 1)
            ch.then(v.tensor_scalar(empty[:], tok_ps, 0.0, 2.0 * T, ALU.is_equal, ALU.mult))
            v.scalar_tensor_tensor(out=slot_idx[:], in0=tok_ps, scalar=-1.0, in1=empty[:],
                                   op0=ALU.add, op1=ALU.add).then_inc(idx_ready, 1)
            ch.then(v.tensor_tensor(col_hot, col_hot, over_e(prob, COLS), ALU.mult))
            v.tensor_tensor(payload[:, :, 2, :], col_hot, payload[:, :, 1, :].bitcast(F32), ALU.subtract) \
                .then_inc(prob_ready, 1)
            ch.then(v.tensor_tensor(over[:], tmp.unsqueeze(1).to_broadcast([P, MAX_OVER, E]),
                                    iota_r[:, 1:1 + MAX_OVER].unsqueeze(2).to_broadcast([P, MAX_OVER, E]),
                                    ALU.is_equal))
            ch.then(v.tensor_tensor(over2[:], over[:], iota_r[:, 0:E].unsqueeze(1).to_broadcast([P, MAX_OVER, E]),
                                    ALU.mult))
            ch.then(v.tensor_reduce(tab[:, 0, E:E + MAX_OVER], over2[:], AX, ALU.add))
            ch.then(v.tensor_tensor(over2[:], over[:], cnt[:, 0, :].unsqueeze(1).to_broadcast([P, MAX_OVER, E]),
                                    ALU.mult))
            ch.then(v.tensor_reduce(tab[:, 2, E:E + MAX_OVER], over2[:], AX, ALU.add))
            ch.done(v.tensor_scalar(tab[:, 2, E:E + MAX_OVER], tab[:, 2, E:E + MAX_OVER], -float(HALF), None,
                                    ALU.add))
            ch.done(v.tensor_scalar(tab[:, 1, E:E + MAX_OVER], tab[:, 0, E:E + MAX_OVER], 2.0 * NSEG, float(NSEG),
                                    ALU.mult, ALU.add))
            ch.then(v.tensor_scalar(tab[:, 3, 0:1], incl[:, E - 1:E], float(E), None, ALU.add))
            ch.then(v.tensor_copy(tab_i[:], tab[:]))

            def ln_stats(p, c):
                n = SLOT_TILES[c]
                wait_apart(dve, gathered[c], 16 * (p + 1), vec_tick)
                ch.done(v.bn_stats(bn[0:n, c, :], xg[0:n, c, :]))

            def ln_var_out():
                wait_apart(dve, chain_s, ch.base + ch.n, vec_tick)
                for c, n in enumerate(SLOT_TILES):
                    ch.done(v.bn_aggr(mv[0:n, c, :], bn[0:n, c, :]))
                ch.wait()
                dve.sem_inc(ln_var, 1)

            def ln_scale(p):
                dve.wait_ge(ln_sd, p + 1)
                rsqrt(rs, mv[:, 0:NSEG, 1], NSEG, sd)
                v.scalar_tensor_tensor(out=rs[:, 0:NSEG, 3], in0=mv[:, 0:NSEG, 0], scalar=-1.0,
                                       in1=rs[:, 0:NSEG, 0], op0=ALU.mult, op1=ALU.mult).then_inc(ln_aff, 1)

            LN_CHAIN = 2 * NSEG + 4

            def xT_copy(p, k):
                dve.wait_ge(xt_hi, KD * p + k + 1)
                v.tensor_tensor(xT_lo[:, k, :], tp[(k + 1) % 2][:, 0:HALF], xT_hi[:, k, :].bitcast(F32),
                                ALU.subtract).then_inc(xt_lo, 1)

            def y_copy(p):
                dve.wait_ge(y_done, NF * p)
                for k in range(2, KD):
                    v.tensor_copy(yT[:, k, :], y_acc[k][:, 0:HALF]).then_inc(yt_vec, 1)

            def final(done, cs):
                for c in cs:
                    n = SLOT_TILES[c]
                    dve.wait_ge(fin_full[c], done)
                    dve.wait_ge(rows_kept, NSEG * done)
                    v.scalar_tensor_tensor(out=xres[0:n, c, :], in0=tp[c % 2][0:n, :], scalar=p_s[0:n, c:c + 1],
                                           in1=xres[0:n, c, :], op0=ALU.mult, op1=ALU.add).then_inc(fin_ready[c], 1)

            for c in range(NSEG):
                ln_stats(0, c)
            ln_var_out()
            dve.wait_ge(prob_done, 1)
            ch.then(v.tensor_copy(slot_p[:], prob_ps[:, 0:COLS]))
            ch.then(v.tensor_tensor(slot_p[:], prob_ps[:, COLS:2 * COLS], slot_p[:], ALU.add))
            dve.wait_ge(idx_ready, 1)
            dve.sem_inc(tab_ready, 1)
            ln_scale(0)
            for k in range(KD):
                xT_copy(0, k)
            n_pass = dve.value_load(tab_i[0:1, 3, 0:1], min_val=E, max_val=E + MAX_OVER)
            start = ch.n
            with dve.Fori(0, n_pass) as p:
                ch.base, ch.n = p * LN_CHAIN, start
                with dve.If(p > 0):
                    y_copy(p)
                with dve.Else():
                    dve.nop()
                for s in range(NF):
                    dve.wait_ge(hh_ready, NF * p + s + 1)
                    v.scalar_tensor_tensor(out=h_lo[:, s % 2, :], in0=row_acc[s % 2][:, 0:HALF], scalar=0.0,
                                           in1=h_hi[:, s % 2, :].bitcast(F32), op0=ALU.max,
                                           op1=ALU.subtract).then_inc(hl_ready, 1)

                    def pieces():
                        for item, js in ring_work(s):
                            for j in js:
                                split_lo(PIECES * (NT + 8 * p + item), item % RING, j)

                    if s in (2, 3):
                        with dve.If(p > 0):
                            final(p, (0, 1) if s == 2 else (2,))
                        with dve.Else():
                            dve.nop()
                    if s < 9:
                        pieces()
                        continue
                    if s < 3 * FC:
                        pieces()
                    with dve.If(p + 1 < n_pass):
                        if s == NF - 1:
                            xT_copy(p + 1, 0)
                            xT_copy(p + 1, 1)
                        if s == 12:
                            ln_scale(p + 1)
                        if s >= 3 * FC:
                            pieces()
                        if s == NF - 1:
                            xT_copy(p + 1, 2)
                            xT_copy(p + 1, 3)
                        if s == 9:
                            ln_stats(p + 1, 0)
                        if s == 10:
                            ln_stats(p + 1, 1)
                            ln_stats(p + 1, 2)
                            ln_var_out()
                    with dve.Else():
                        dve.nop()
                dve.nop()
            y_copy(n_pass)
            final(n_pass, range(NSEG))

        @block.tensor
        def _(pe):
            mm = nc.tensor.matmul
            pe.wait_ge(consts, 1)
            for i in range(2):
                pe.wait_ge(w_stat_ready, i + 1)
                src = mv_w[:, i, 0:1]
                mm(stat_ps[:, i:i + 1], mean_w[:], src, start=True, stop=True).then_inc(stat_mm, 1)
            pe.wait_ge(need_ready, 1)
            need = pe.value_load(need_lo[0:1, 0:1], min_val=0, max_val=1)

            def support(u, parts):
                for k in range(KD):
                    for part in parts:
                        last = mm(row_acc[u % 2][:], part[:, u % 2, k * P:(k + 1) * P], wq[:, k, :],
                                  start=(k == 0 and part is qT_hi), stop=(k == KD - 1 and part is parts[-1]))
                last.then_inc(acc_full, 1)

            for t in range(NT + 1):
                if t < NT:
                    pe.wait_ge(q_ready, t + 1)
                    pe.wait_ge(tp_free, t + 1)
                    for k in range(KD):
                        last = nc.tensor.transpose(tp[t % 2][:, k * P:(k + 1) * P],
                                                   q[:, t % 2, k * P:(k + 1) * P], ident[:])
                    last.then_inc(tp_full, 1)
                if t == 1:
                    pe.wait_ge(wq_ready, 1)
                if t >= 1:
                    u = t - 1
                    pe.wait_ge(tp_free, 2 + u + 1)
                    if u >= 2:
                        pe.wait_ge(sup_ready, u - 1)
                    with pe.If(need > 0):
                        support(u, (qT_hi, qT_lo))
                    with pe.Else():
                        support(u, (qT_hi,))

            def gate_in(step, b):
                pe.wait_ge(xn1_ready, step)
                for k in range(KD):
                    last = nc.tensor.transpose(tp[b][:, k * P:(k + 1) * P], xn1[:, k * P:(k + 1) * P], ident[:])
                last.then_inc(tp_full, 1)

            def gate_out(step):
                pe.wait_ge(xn1T_ready, step)
                dst = logit_cols[:, bass.ds(step, 1), :].rearrange("p a e -> p (a e)")
                for k in range(KD):
                    last = mm(dst, xn1T[:, k, :], gate[:, k, :], start=(k == 0), stop=(k == KD - 1))
                last.then_inc(gate_done, 1)

            def adj_rows(t, j, jts, stop):
                for jt in jts:
                    for part in (hi, lo):
                        last = mm(row_acc[j % 2][:], part[:, j, jt * P:(jt + 1) * P], S[:, jt, :],
                                  start=(jt == 0 and part is hi), stop=(jt == NT - 1 and part is lo))
                if stop:
                    last.then_inc(acc_full, 1)

            def group_b(g, last):
                for j in range(4):
                    t = 4 * g + j
                    pe.wait_ge(lo_ready, PIECES * (t + 1))
                    adj_rows(t, j, range(10), False)
                    if j == 0 and not last:
                        with pe.If(g > 0):
                            gate_in(t, 1)
                        with pe.Else():
                            pe.nop()
                    else:
                        gate_in(t, (j - 1) % 2)
                    adj_rows(t, j, range(10, NT), True)
                    if j == 0 and not last:
                        with pe.If(g > 0):
                            gate_out(t)
                        with pe.Else():
                            pe.nop()
                    else:
                        gate_out(t)

            pe.wait_ge(S_ready, NT)
            with pe.Fori(0, 3) as g:
                group_b(g, False)
            group_b(3, True)
            gate_in(NT, 1)
            gate_out(NT)

            pe.wait_ge(mask_ready, 1)
            mflat = mask[:].rearrange("p t e -> p (t e)")
            mm(prefix, tri[:], mflat, start=True, stop=False)
            for sh in range(1, NT):
                last = mm(prefix[:, sh * E:NT * E], ones_b[:], mflat[:, 0:(NT - sh) * E], start=False,
                          stop=(sh == NT - 1))
            last.then_inc(pos_ready, 1)
            for t in range(NT):
                last = mm(counts_ps, ones_b[:], mask[:, t, :], start=(t == 0), stop=(t == NT - 1))
            last.then_inc(counts_done, 1)

            def by_slot(dst, payloads):
                for t in range(NT):
                    if t % (NT // 2) == 0:
                        pe.wait_ge(r_hot_ready, t // (NT // 2) + 1)
                    last = mm(dst, r_hot[:, t, :], payload[:, t, payloads, :].rearrange("p j c -> p (j c)"),
                              start=(t == 0), stop=(t == NT - 1))
                return last

            pe.wait_ge(tok_ready, 1)
            by_slot(tok_ps, slice(0, 1)).then_inc(tok_done, 1)
            pe.wait_ge(prob_ready, 1)
            by_slot(prob_ps, slice(1, 3)).then_inc(prob_done, 1)


            def xT(p, k):
                pe.wait_ge(xn2_ready, NSEG * (p + 1))
                if k >= 2:
                    pe.wait_ge(xt_lo, KD * p + k - 1)
                at = 0
                for c, n in enumerate(SLOT_TILES):
                    last = nc.tensor.transpose(tp[(k + 1) % 2][:, at:at + n], xn2[0:n, c, k * P:(k + 1) * P],
                                               ident[0:n, 0:n])
                    at += n
                last.then_inc(xt_full, 1)

            def final(done, c):
                if c == 0:
                    pe.wait_ge(yt_act, 2 * done)
                    pe.wait_ge(yt_vec, 2 * done)
                if c >= 2:
                    pe.wait_ge(fin_ready[c - 2], done)
                for k in range(KD):
                    at = k * HALF + c * P
                    last = nc.tensor.transpose(tp[c % 2][:, k * P:(k + 1) * P], yT_flat[:, at:at + P], ident[:])
                last.then_inc(fin_full[c], 1)

            def up(p, s, w):
                item = 2 * (s // FC)
                if s % FC == 0:
                    pe.wait_ge(lo_ready, PIECES * (NT + 8 * p + item + 1))
                if s >= 2:
                    pe.wait_ge(hl_ready, NF * p + s - 1)
                for k in range(KD):
                    if s == 0:
                        pe.wait_ge(xt_lo, KD * p + k + 1)
                    at = k * FC * P + (s % FC) * P
                    for i, (a, b) in enumerate(((hi, xT_hi), (hi, xT_lo), (lo, xT_hi))):
                        last = mm(row_acc[s % 2][:, 0:w], a[:, item % RING, at:at + P], b[:, k, 0:w],
                                  start=(k == 0 and i == 0), stop=(k == KD - 1 and i == 2))
                last.then_inc(h_full, 1)

            def down(p, s, w):
                item = 2 * (s // FC) + 1
                if s % FC == 0:
                    pe.wait_ge(lo_ready, PIECES * (NT + 8 * p + item + 1))
                pe.wait_ge(hl_ready, NF * p + s + 1)
                for k in range(KD):
                    at = (s % FC) * D + k * P
                    for i, (a, b) in enumerate(((hi, h_hi), (hi, h_lo), (lo, h_hi))):
                        last = mm(y_acc[k][:, 0:w], a[:, item % RING, at:at + P], b[:, s % 2, 0:w],
                                  start=(s == 0 and i == 0), stop=(s == NF - 1 and i == 2))
                last.then_inc(y_done, 1)

            def expert_pass(p, w):
                for s in range(NF):
                    if s == NF - 1:
                        with pe.If(p + 1 < n_pass):
                            pe.wait_ge(rotated, 2 * NSEG * (p + 1))
                            xT(p + 1, 0)
                            xT(p + 1, 1)
                        with pe.Else():
                            pe.nop()
                    up(p, s, w)
                    if s in (1, 2, 3):
                        with pe.If(p > 0):
                            if s == 1:
                                pe.wait_ge(yt_act, 2 * p)
                                pe.wait_ge(yt_vec, 2 * p)
                                pe.nop()
                            for c in {1: (), 2: (0, 1), 3: (2,)}[s]:
                                final(p, c)
                        with pe.Else():
                            pe.nop()
                    if s >= 1:
                        down(p, s - 1, w)
                down(p, NF - 1, w)
                with pe.If(p + 1 < n_pass):
                    xT(p + 1, 2)
                    xT(p + 1, 3)
                with pe.Else():
                    pe.nop()

            for k in range(KD):
                xT(0, k)
            pe.wait_ge(tab_ready, 1)
            n_pass = pe.value_load(tab_i[0:1, 3, 0:1], min_val=E, max_val=E + MAX_OVER)
            with pe.Fori(0, n_pass) as p:
                n_tok = pe.value_load(tab_i[0:1, 2, bass.ds(p, 1)])

                def narrowest(i):
                    if i == len(WIDTHS) - 1:
                        expert_pass(p, WIDTHS[i])
                        return
                    with pe.If(n_tok <= WIDTHS[i]):
                        expert_pass(p, WIDTHS[i])
                    with pe.Else():
                        narrowest(i + 1)
                    pe.nop()

                narrowest(0)
            for c in range(NSEG):
                final(n_pass, c)


def kernel(**inputs):
    import numpy as np
    import concourse.bacc as bacc
    from concourse import mybir as mb
    from concourse.bass_utils import run_bass_kernel_spmd

    f = {k: np.asarray(a) for k, a in inputs.items()}
    arrays = {
        "x_rows": f["x"].reshape(NT, P, D).transpose(1, 0, 2),
        "adj_tiles": f["adj"].reshape(NT, P, NT, P).transpose(0, 3, 2, 1).reshape(NT, P, ITEM),
        "gnn_weight": f["L0_gnn_weight"].reshape(KD, P, D).transpose(1, 0, 2),
        "scales": np.broadcast_to(np.stack([f["L0_gnn_" + k].reshape(()) for k in (
            "adj_scaling_factor", "wgt_alpha", "act_alpha", "act_alpha2", "act_alpha2")]), (P, 5)),
        "gate_w": f["L0_ffn_gate_w"].reshape(KD, P, E).transpose(1, 0, 2),
        "experts": np.stack([
            f["L0_ffn_w1"].reshape(E, KD, P, NC, FC * P).transpose(0, 3, 2, 1, 4).reshape(E, NC, P, ITEM),
            f["L0_ffn_w2"].reshape(E, NC, FC, P, D).transpose(0, 1, 3, 2, 4).reshape(E, NC, P, ITEM),
        ], axis=2).reshape(E * NC * 2, P, ITEM),
    }
    arrays = {k: np.ascontiguousarray(a) for k, a in arrays.items()}
    nc = bacc.Bacc("TRN2", target_bir_lowering=False, num_devices=1)
    ins = [nc.dram_tensor(k, a.shape, mb.dt.from_np(a.dtype), kind="ExternalInput").ap()
           for k, a in arrays.items()]
    out = nc.dram_tensor("out_rows", (T, D), mb.dt.float32, kind="ExternalOutput").ap()
    x1_rows = nc.dram_tensor("x1_rows", (T, D), mb.dt.float32, kind="Internal").ap()
    gnn_moe_kernel(nc, ins[0], ins[1], ins[2], ins[3], ins[4], ins[5], out, x1_rows)
    r = run_bass_kernel_spmd(nc, [arrays], core_ids=[0])
    return r.results[0]["out_rows"]
```

```python
from contextlib import ExitStack

import concourse.bass as bass
from concourse import mybir

P = 128
T, D, E, F, CAP = 2048, 512, 8, 2048, 640
NT = T // P
KD = D // P
NF = F // P
FC = 4
NC = NF // FC
HALF = CAP // 2
SLOT_TILES = [P, P, HALF - 2 * P]
NSEG = len(SLOT_TILES)
MAX_OVER = T // (HALF + 1)
NPT = E + MAX_OVER + 2
COLS = E * 2 * NSEG
WIDTHS = list(range(256, HALF, 8)) + [HALF]
ITEM = NT * P
RING = 4
PIECES = 4
PIECE = ITEM // PIECES
MAGIC = 12582912.0
EPS = 1e-5
ACT_N = 15.0
WGT_N = 7.0
STEP_A = 4
HEAD = RING - 1
EARLY = NT - RING
HEAD_LAG = 5
CODE_MAX = 4095.0
KEEP_AT = [5, 6, 8]

ALU = mybir.AluOpType
ACT = mybir.ActivationFunctionType
AX = mybir.AxisListType.X
F32 = mybir.dt.float32
F32R = mybir.dt.float32r
BF16 = mybir.dt.bfloat16
I32 = mybir.dt.int32


class Chain:

    def __init__(self, engine, sem):
        self.engine, self.sem, self.n, self.base = engine, sem, 0, 0

    def done(self, ins):
        ins.then_inc(self.sem, 1)
        self.n += 1

    def wait(self):
        self.engine.wait_ge(self.sem, self.base + self.n)

    def then(self, ins):
        self.done(ins)
        self.wait()


def wait_apart(engine, sem, value, tick):
    engine.wait_ge(sem, value)
    engine.sem_inc(tick, 1)


def gnn_moe_kernel(nc, x_in, adj_in, w_in, scal_in, gate_in, experts_in, out, x1_rows):
    with ExitStack() as ctx:
        def sb(name, shape, dt):
            return ctx.enter_context(nc.sbuf_tensor(name, shape, dt))

        def psum(name):
            return ctx.enter_context(nc.psum_tensor(name, [P, 512], F32))

        def sem(name):
            return ctx.enter_context(nc.semaphore(name))

        raw = sb("raw", [P, RING, ITEM], F32)
        hi = sb("hi", [P, RING, ITEM], F32R)
        lo = sb("lo", [P, RING, ITEM], F32R)
        x = sb("x", [P, NT, D], F32)
        S = sb("S", [P, NT, D], F32R)
        fr = sb("fr", [P, 8 * 512], F32R)
        fb = sb("fb", [P, 3 * NSEG * D + KD * HALF + P - SLOT_TILES[-1]], F32)

        wq = fr[:, 0:KD * D].rearrange("p (k n) -> p k n", k=KD)
        qT_hi = fr[:, 2048:3072].rearrange("p (b n) -> p b n", b=2)
        qT_lo = fr[:, 3072:4096].rearrange("p (b n) -> p b n", b=2)
        wraw = fb[:, 0:KD * D].rearrange("p (k n) -> p k n", k=KD)
        q = fb[:, 2048:3072].rearrange("p (b n) -> p b n", b=2)
        sup = fb[:, 3072:4096].rearrange("p (b n) -> p b n", b=2)
        xn1 = fb[:, 4096:4608]
        xn_head = fb[:, 2048:2048 + HEAD * D].rearrange("p (t n) -> p t n", t=HEAD)
        xn1T = fb[:, 4608:5120].rearrange("p (k n) -> p k n", k=KD)
        r_hot = fr[:, 0:NT * P].rearrange("p (t r) -> p t r", t=NT)
        tok_by_col = fr[:, NT * P:NT * (P + COLS)].rearrange("p (t c) -> p t c", t=NT)
        prob_by_col = S[:, 0:3, :].rearrange("p a b -> p (a b)")[:, 0:NT * 2 * COLS] \
            .rearrange("p (t j c) -> p t j c", t=NT, j=2)
        col_hot = fb[:, 2048:2048 + NT * COLS].rearrange("p (t c) -> p t c", t=NT)
        xT_hi = fr[:, 0:KD * HALF].rearrange("p (k n) -> p k n", k=KD)
        xT_lo = fr[:, KD * HALF:2 * KD * HALF].rearrange("p (k n) -> p k n", k=KD)
        h_hi = fr[:, 8 * HALF:10 * HALF].rearrange("p (b n) -> p b n", b=2)
        h_lo = fr[:, 10 * HALF:12 * HALF].rearrange("p (b n) -> p b n", b=2)
        seg = NSEG * D
        xg = fb[:, 0:seg].rearrange("p (c n) -> p c n", c=NSEG)
        xres = fb[:, seg:2 * seg].rearrange("p (c n) -> p c n", c=NSEG)
        xn2 = fb[:, 2 * seg:3 * seg].rearrange("p (c n) -> p c n", c=NSEG)
        yT_flat = fb[:, 3 * seg:]
        yT = yT_flat[:, 0:KD * HALF].rearrange("p (k n) -> p k n", k=KD)

        ident = sb("ident", [P, P], F32)
        tri = sb("tri", [P, P], BF16)
        ones_b = sb("ones_b", [P, P], BF16)
        mean_w = sb("mean_w", [P, P], F32)
        scal = sb("scal", [P, 5], F32)
        con = sb("con", [P, 16], F32)
        gate = sb("gate", [P, KD, E], F32)
        bn = sb("bn", [P, 4, 6], F32)
        mv = sb("mv", [P, 4, 2], F32)
        sd = sb("sd", [P, 4], F32)
        bn_w = sb("bn_w", [P, KD, 6], F32)
        mv_w = sb("mv_w", [P, 2, 2], F32)
        w_dev = sb("w_dev", [P, 1], F32)
        w_off = sb("w_off", [P, 1], F32)
        need_f = sb("need_f", [P, 1], F32)
        need_lo = sb("need_lo", [P, 1], I32)
        rs = sb("rs", [P, 4, 4], F32)
        aff = sb("aff", [P, 2, STEP_A, 4], F32)
        iota_i = sb("iota_i", [P, P], I32)
        iota_r = sb("iota_r", [P, P], F32)
        rev_i = sb("rev_i", [P, NT], I32)
        tok1 = sb("tok1", [P, NT], F32)
        lgs = sb("lgs", [P, NT, E], F32)
        ex = sb("ex", [P, NT, E], F32)
        key = sb("key", [P, NT, E], F32)
        mask = sb("mask", [P, NT, E], BF16)
        rev_e = sb("rev_e", [P, E], F32)
        small = sb("small", [P, 11, NT], F32)
        cnt = sb("cnt", [P, 6, E], F32)
        over = sb("over", [P, MAX_OVER, E], F32)
        over2 = sb("over2", [P, MAX_OVER, E], F32)
        tab = sb("tab", [P, 4, NPT], F32)
        tab_i = sb("tab_i", [P, 4, NPT], I32)
        empty = sb("empty", [P, COLS], F32)
        slot_idx = sb("slot_idx", [P, COLS], I32)
        slot_p = sb("slot_p", [P, COLS], F32)
        idx_g = sb("idx_g", [P, NSEG], I32)
        idx_s = sb("idx_s", [P, NSEG], I32)
        p_g = sb("p_g", [P, NSEG], F32)
        p_s = sb("p_s", [P, NSEG], F32)

        row_acc = [psum("row_acc0"), psum("row_acc1")]
        y_acc = [psum(f"y_acc{k}") for k in range(KD)]
        tp = [psum("tp0"), psum("tp1")]
        logit_cols, late_cols = (y_acc[k][:, 0:(NT + 1) * E].rearrange("p (t e) -> p t e", t=NT + 1)
                                 for k in (0, KD - 1))
        logits, late_logits = logit_cols[:, 1:NT + 1, :], late_cols[:, 1:NT + 1, :]
        prefix = y_acc[1][:, 0:NT * E]
        tok_ps = y_acc[2][:, 0:COLS]
        prob_ps = row_acc[0][:, 0:2 * COLS]
        counts_ps = y_acc[3][:, 0:E]
        stat_ps = y_acc[3][:, 16:18]

        inv_asf, k_x, k_w, k_sup, k_sq, k_out, eps_c, neg_magic, w_mean, w_scale = (
            con[:, i:i + 1] for i in range(10))

        small_in = sem("small_in")
        w_in_sem = sem("w_in_sem")
        x_in_sem = [sem(f"x_in{g}") for g in range(4)]
        raw_in = [sem(f"raw_in{s}") for s in range(RING)]
        hi_ready = sem("hi_ready")
        lo_ready = sem("lo_ready")
        consts = sem("consts")
        chain_s = sem("vec_chain")
        achain_s = sem("act_chain")
        pool_s = sem("pool_chain")
        pool_tick = sem("pool_tick")
        vec_tick = sem("vec_tick")
        scal_ready = sem("scal_ready")
        need_ready = sem("need_ready")
        w_stat_ready = sem("w_stat_ready")
        stat_mm = sem("stat_mm")
        wq_ready = sem("wq_ready")
        var_ready = sem("var_ready")
        sd_ready = sem("sd_ready")
        aff_ready = sem("aff_ready")
        xn_ready = sem("xn_ready")
        q_ready = sem("q_ready")
        tp_full = sem("tp_full")
        tp_free = sem("tp_free")
        qT_hi_ready = sem("qT_hi_ready")
        acc_full = sem("acc_full")
        sup_ready = sem("sup_ready")
        S_ready = sem("S_ready")
        x1_ready = sem("x1_ready")
        xn1_ready = sem("xn1_ready")
        xn1T_ready = sem("xn1T_ready")
        gate_done = sem("gate_done")
        rows_out = sem("rows_out")
        shift_ready = sem("shift_ready")
        exp_ready = sem("exp_ready")
        mask_ready = sem("mask_ready")
        pos_ready = sem("pos_ready")
        tok_ready = sem("tok_ready")
        prob_ready = sem("prob_ready")
        r_hot_ready = sem("r_hot_ready")
        tok_done = sem("tok_done")
        idx_ready = sem("idx_ready")
        counts_done = sem("counts_done")
        prob_done = sem("prob_done")
        tab_ready = sem("tab_ready")
        staged = sem("staged")
        gathered = [sem(f"gathered{c}") for c in range(NSEG)]
        rows_kept = sem("rows_kept")
        ln_var = sem("ln_var")
        ln_sd = sem("ln_sd")
        ln_aff = sem("ln_aff")
        xn2_ready = sem("xn2_ready")
        xt_full = sem("xt_full")
        xt_hi = sem("xt_hi")
        xt_lo = sem("xt_lo")
        h_full = sem("h_full")
        hh_ready = sem("hh_ready")
        hl_ready = sem("hl_ready")
        y_done = sem("y_done")
        yt_act = sem("yt_act")
        yt_vec = sem("yt_vec")
        fin_full = [sem(f"fin_full{c}") for c in range(NSEG)]
        rotated = sem("rotated")
        fin_ready = [sem(f"fin_ready{c}") for c in range(NSEG)]
        scattered = [sem(f"scattered{c}") for c in range(NSEG)]

        def piece(buf, slot, j):
            return buf[:, slot, j * PIECE:(j + 1) * PIECE]

        def first_items(t):
            k = t - 2
            if 0 <= k < HEAD * PIECES:
                return [(k % HEAD, k // HEAD)]
            return [(HEAD, k - HEAD * PIECES)] if HEAD * PIECES <= k < RING * PIECES else []

        def ring_work(s):
            if s < 3 * FC:
                return [(2 + s // 2, (0, 1) if s % 2 == 0 else (2, 3))]
            return {12: [(8, (0, 1, 2))], 13: [(8, (3,)), (9, (0,))], 14: [(9, (1, 2))], 15: [(9, (3,))]}[s]

        block = ctx.enter_context(nc.Block())

        @block.sync
        def _(sp):
            sp.dma_start(scal[:], scal_in).then_inc(small_in, 16)
            sp.dma_start(gate[:], gate_in).then_inc(small_in, 16)
            for g in range(4):
                sp.dma_start(x[:, 4 * g:4 * g + 4, :], x_in[:, 4 * g:4 * g + 4, :]).then_inc(x_in_sem[g], 16)
                if g == 0:
                    sp.dma_start(wraw, w_in).then_inc(w_in_sem, 16)
            for n in range(RING):
                sp.dma_start(raw[:, n, :], adj_in[n]).then_inc(raw_in[n], 16)
            sp.wait_ge(hi_ready, HEAD * PIECES)
            sp.wait_ge(lo_ready, HEAD * PIECES)
            with sp.Fori(1, NT // RING) as g:
                for s in range(RING):
                    sp.wait_ge(hi_ready, PIECES * (RING * g + s - RING + 1))
                    sp.wait_ge(lo_ready, PIECES * (RING * g + s - RING + 1))
                    sp.dma_start(raw[:, s, :], adj_in[bass.ds(RING * g + s, 1)].rearrange("a p n -> (a p) n")).then_inc(raw_in[s], 16)

            def load_pass(p, e):
                for i in range(2 * NC):
                    first = NT + 8 * p + i - RING + 1
                    sp.wait_ge(hi_ready, PIECES * first)
                    sp.wait_ge(lo_ready, PIECES * first)
                    sp.dma_start(raw[:, i % RING, :], experts_in[bass.ds(e * (2 * NC) + i, 1)].rearrange("a p n -> (a p) n")) \
                        .then_inc(raw_in[i % RING], 16)

            with sp.Fori(0, E) as p:
                load_pass(p, p)
            sp.wait_ge(tab_ready, 1)
            n_pass = sp.value_load(tab_i[0:1, 3, 0:1], min_val=E, max_val=E + MAX_OVER)
            with sp.If(n_pass > E):
                with sp.Fori(E, n_pass) as p:
                    e = sp.value_load(tab_i[0:1, 0, bass.ds(p, 1)], min_val=0, max_val=E - 1)
                    load_pass(p, e)

        @block.gpsimd
        def _(pool):
            ch = Chain(pool, pool_s)
            ch.done(nc.gpsimd.memset(ident[:], 0.0))
            ch.done(nc.gpsimd.memset(tri[:], 1.0))
            ch.done(nc.gpsimd.memset(ones_b[:], 1.0))
            ch.done(nc.gpsimd.memset(mean_w[:], 1.0 / P))
            ch.done(nc.gpsimd.iota(iota_i[:], pattern=[[1, P]], base=0, channel_multiplier=0))
            ch.done(nc.gpsimd.iota(rev_i[:], pattern=[[P, NT]], base=1, channel_multiplier=1))
            ch.wait()
            ch.done(nc.gpsimd.affine_select(out=ident[:], in_=ident[:], compare_op=ALU.not_equal, fill=1.0,
                                            base=0, pattern=[[-1, P]], channel_multiplier=1))
            ch.done(nc.gpsimd.affine_select(out=tri[:], in_=tri[:], compare_op=ALU.is_gt, fill=0.0,
                                            base=0, pattern=[[1, P]], channel_multiplier=-1))
            ch.done(nc.gpsimd.tensor_copy(iota_r[:], iota_i[:]))
            ch.done(nc.gpsimd.tensor_copy(tok1[:], rev_i[:]))
            ch.wait()
            pool.sem_inc(consts, 1)
            pool.wait_ge(wq_ready, 1)
            ch.then(nc.gpsimd.memset(xg[:, 0:NSEG, :], 0.0))

            def gather_dma(c, n):
                nc.gpsimd.indirect_dma_start(
                    out=xg[0:n, c, :], out_offset=None, in_=x1_rows[:, :],
                    in_offset=bass.IndirectOffsetOnAxis(ap=idx_g[0:n, c:c + 1], axis=0),
                    bounds_check=T - 1, oob_is_err=False).then_inc(gathered[c], 16)

            with pool.Fori(0, NT) as t:
                pool.wait_ge(x1_ready, t + 1)
                src = x[:, bass.ds(t, 1), :].rearrange("p a n -> p (a n)")
                pool.dma_start(x1_rows[bass.ds(t * P, P), :], src).then_inc(rows_out, 16)
                pool.dma_start(out[bass.ds(t * P, P), :], src).then_inc(rows_out, 16)

            pool.wait_ge(rows_out, 32 * NT)
            pool.wait_ge(idx_ready, 1)
            nc.gpsimd.tensor_copy(idx_g[:], slot_idx[:, 0:NSEG]).then_inc(staged, NSEG)
            pool.wait_ge(staged, NSEG)
            for c, n in enumerate(SLOT_TILES):
                gather_dma(c, n)
            pool.wait_ge(tab_ready, 1)
            nc.gpsimd.tensor_copy(p_g[:], slot_p[:, 0:NSEG]).then_inc(staged, NSEG)
            pool.wait_ge(staged, 2 * NSEG)
            n_pass = pool.value_load(tab_i[0:1, 3, 0:1], min_val=E, max_val=E + MAX_OVER)

            def gather(p, c):
                n = SLOT_TILES[c]
                col = pool.value_load(tab_i[0:1, 1, bass.ds(p, 1)], min_val=0, max_val=COLS - NSEG)
                nc.gpsimd.tensor_copy(idx_g[:, c:c + 1], slot_idx[:, bass.ds(col + c, 1)]).then_inc(staged, 1)
                nc.gpsimd.tensor_copy(p_g[:, c:c + 1], slot_p[:, bass.ds(col + c, 1)]).then_inc(staged, 1)
                wait_apart(pool, staged, 2 * NSEG * p + 2 * (c + 1), pool_tick)
                gather_dma(c, n)

            def scatter(done, c):
                n = SLOT_TILES[c]
                wait_apart(pool, fin_ready[c], done, pool_tick)
                nc.gpsimd.indirect_dma_start(
                    out=out[:, :], out_offset=bass.IndirectOffsetOnAxis(ap=idx_s[0:n, c:c + 1], axis=0),
                    in_=xres[0:n, c, :], in_offset=None,
                    bounds_check=T - 1, oob_is_err=False).then_inc(scattered[c], 16)

            def rotate(p, c):
                nc.gpsimd.tensor_copy(idx_s[:, c:c + 1], idx_g[:, c:c + 1]).then_inc(rotated, 1)
                nc.gpsimd.tensor_copy(p_s[:, c:c + 1], p_g[:, c:c + 1]).then_inc(rotated, 1)
                wait_apart(pool, rotated, 2 * NSEG * p + 2 * (c + 1), pool_tick)

            def gather_next(p, c):
                with pool.If(p + 1 < n_pass):
                    wait_apart(pool, rows_kept, NSEG * p + c + 1, pool_tick)
                    gather(p + 1, c)
                    pool.nop()

            with pool.Fori(0, n_pass) as p:
                for c in range(NSEG):
                    with pool.If(p > 0):
                        scatter(p, c)
                        pool.nop()
                    if c >= 1:
                        gather_next(p, c - 1)
                    with pool.If(p > 0):
                        wait_apart(pool, scattered[c], 16 * p, pool_tick)
                    rotate(p, c)
                gather_next(p, NSEG - 1)
            for c in range(NSEG):
                scatter(n_pass, c)
            for c in range(NSEG):
                wait_apart(pool, scattered[c], 16 * n_pass, pool_tick)

        @block.scalar
        def _(act):
            ch = Chain(act, achain_s)

            def split_hi(n_ready, slot, j, scale=None):
                if j == 0:
                    act.wait_ge(raw_in[slot], n_ready)
                nc.scalar.activation(piece(hi, slot, j), piece(raw, slot, j), ACT.Copy if scale is None else
                                     ACT.Identity, scale=1.0 if scale is None else scale).then_inc(hi_ready, 1)

            def row_stats(g):
                act.wait_ge(var_ready, g + 1)
                nc.scalar.activation(sd[:], mv[:, :, 1], ACT.Sqrt, bias=eps_c).then_inc(sd_ready, 1)

            row_stats(0)
            act.wait_ge(stat_mm, 2)
            act.wait_ge(scal_ready, 1)
            nc.scalar.activation(w_dev[:], stat_ps[:, 1:2], ACT.Sqrt, scale=float(D * D) / (D * D - 1)) \
                .then_inc(sd_ready, 1)
            for t in range(NT + 2):
                if t < NT:
                    g = t // STEP_A
                    act.wait_ge(aff_ready, g + 1)
                    if t >= 2:
                        act.wait_ge(tp_full, t - 1)
                    nc.scalar.activation(q[:, t % 2, :], x[:, t, :], ACT.Identity,
                                         scale=aff[:, g % 2, t % 4, 2:3], bias=aff[:, g % 2, t % 4, 3:4]) \
                        .then_inc(xn_ready, 1)
                if 1 <= t <= NT:
                    act.wait_ge(tp_full, t)
                    if t >= 3:
                        act.wait_ge(acc_full, t - 2)
                    nc.scalar.activation(qT_hi[:, (t - 1) % 2, :], tp[(t - 1) % 2][:], ACT.Identity,
                                         bias=neg_magic).then_inc(qT_hi_ready, 1)
                if t >= 2:
                    act.wait_ge(acc_full, t - 1)
                    if t >= 4:
                        act.wait_ge(S_ready, t - 3)
                    nc.scalar.activation(sup[:, t % 2, :], row_acc[t % 2][:], ACT.Relu, scale=k_sup) \
                        .then_inc(sup_ready, 1)
                for item, j in first_items(t):
                    split_hi(16, item, j, inv_asf)
                if t % STEP_A == 2 and t + 2 < NT:
                    row_stats((t + 2) // STEP_A)

            def xn1T_copy(step, b):
                act.wait_ge(tp_full, NT + step)
                nc.scalar.activation(xn1T, tp[b][:].rearrange("p (k n) -> p k n", k=KD), ACT.Copy) \
                    .then_inc(xn1T_ready, 1)

            def sd_rows(t):
                act.wait_ge(var_ready, NT // STEP_A + t + 1)
                nc.scalar.activation(sd[:, 0:1], mv[:, 0, 1:2], ACT.Sqrt, bias=eps_c).then_inc(sd_ready, 1)

            def group_b(g, last):
                for j in range(RING):
                    t = RING * g + j
                    slot = (j + 3) % RING
                    turn = g if j < 1 else g + 1
                    if not (last and j == 3):
                        act.wait_ge(acc_full, NT + t)
                        for i in range(PIECES):
                            split_hi(16 * (turn + 1), slot, i, None if last and j >= 1 else inv_asf)
                    xn1T_copy(t, (j - 1) % 2)
                    sd_rows(t)

            def next_item(slot):
                for i in range(PIECES):
                    split_hi(32, slot, i, inv_asf)

            act.wait_ge(acc_full, NT + HEAD)
            next_item(0)
            act.wait_ge(var_ready, NT // STEP_A + HEAD)
            nc.scalar.activation(sd[:, 0:HEAD], mv[:, 0:HEAD, 1], ACT.Sqrt, bias=eps_c).then_inc(sd_ready, HEAD)
            next_item(1)
            for step in range(1, HEAD + 1):
                xn1T_copy(step, (step - 1) % 2)
            sd_rows(HEAD)
            next_item(2)
            with act.Fori(1, 3) as g:
                group_b(g, False)
            group_b(3, True)
            xn1T_copy(NT, 1)

            act.wait_ge(shift_ready, 2)
            nc.scalar.activation(ex[:], lgs[:], ACT.Exp).then_inc(exp_ready, 1)


            def ln_rows(p):
                act.wait_ge(ln_var, p + 1)
                nc.scalar.activation(sd[:, 0:NSEG], mv[:, 0:NSEG, 1], ACT.Sqrt, bias=eps_c).then_inc(ln_sd, 1)

            def xT_copy(p, k):
                act.wait_ge(xt_full, KD * p + k + 1)
                nc.scalar.activation(xT_hi[:, k, :], tp[(k + 1) % 2][:, 0:HALF], ACT.Copy).then_inc(xt_hi, 1)

            def ln_out(p, cs):
                for c in cs:
                    n = SLOT_TILES[c]
                    act.wait_ge(ln_aff, p + 1)
                    nc.scalar.activation(xn2[0:n, c, :], xg[0:n, c, :], ACT.Identity, scale=rs[0:n, c, 0:1],
                                         bias=rs[0:n, c, 3:4]).then_inc(xn2_ready, 1)

            ln_rows(0)
            ln_out(0, (0, 2))
            for k in range(KD):
                xT_copy(0, k)
            act.wait_ge(tab_ready, 1)
            n_pass = act.value_load(tab_i[0:1, 3, 0:1], min_val=E, max_val=E + MAX_OVER)
            with act.Fori(0, n_pass) as p:
                with act.If(p > 0):
                    act.wait_ge(y_done, NF * p)
                    for k in range(2):
                        nc.scalar.activation(yT[:, k, :], y_acc[k][:, 0:HALF], ACT.Copy).then_inc(yt_act, 1)
                with act.Else():
                    act.nop()
                for s in range(NF):
                    act.wait_ge(h_full, NF * p + s + 1)
                    if s >= 2:
                        act.wait_ge(y_done, NF * p + s - 1)
                    nc.scalar.activation(h_hi[:, s % 2, :], row_acc[s % 2][:, 0:HALF], ACT.Relu) \
                        .then_inc(hh_ready, 1)

                    def pieces():
                        for item, js in ring_work(s):
                            for j in js:
                                split_hi(16 * (4 + 2 * p + item // RING + 1), item % RING, j)

                    if s < 3 * FC:
                        pieces()
                    else:
                        with act.If(p + 1 < n_pass):
                            if s == NF - 1:
                                xT_copy(p + 1, 0)
                                xT_copy(p + 1, 1)
                            if s in (13, 14):
                                ln_out(p + 1, (0, 1) if s == 13 else (2,))
                            pieces()
                            if s == NF - 1:
                                xT_copy(p + 1, 2)
                                xT_copy(p + 1, 3)
                        with act.Else():
                            act.nop()
                    if s == 11:
                        with act.If(p + 1 < n_pass):
                            ln_rows(p + 1)
                        with act.Else():
                            act.nop()
                    if s in KEEP_AT:
                        c = KEEP_AT.index(s)
                        act.wait_ge(rotated, 2 * NSEG * p + 2 * (c + 1))
                        act.wait_ge(gathered[c], 16 * (p + 1))
                        nc.scalar.activation(xres[:, c, :], xg[:, c, :], ACT.Copy).then_inc(rows_kept, 1)
                act.nop()
            act.wait_ge(y_done, NF * n_pass)
            for k in range(2):
                nc.scalar.activation(yT[:, k, :], y_acc[k][:, 0:HALF], ACT.Copy).then_inc(yt_act, 1)

        @block.vector
        def _(dve):
            ch = Chain(dve, chain_s)
            v = nc.vector

            def split_lo(done, slot, j, scale=None):
                dve.wait_ge(hi_ready, done + j + 1)
                a, b = piece(raw, slot, j), piece(hi, slot, j).bitcast(F32)
                if scale is None:
                    v.tensor_tensor(piece(lo, slot, j), a, b, ALU.subtract).then_inc(lo_ready, 1)
                else:
                    v.scalar_tensor_tensor(out=piece(lo, slot, j), in0=a, scalar=scale, in1=b, op0=ALU.mult,
                                           op1=ALU.subtract).then_inc(lo_ready, 1)

            def rsqrt(r, var, n, dev):
                root, tmp = r[:, 0:n, 0], r[:, 0:n, 1]
                ch.then(v.reciprocal(root, dev[:, 0:n]))
                ch.then(v.scalar_tensor_tensor(out=tmp, in0=var, scalar=EPS, in1=root, op0=ALU.add, op1=ALU.mult))
                ch.then(v.scalar_tensor_tensor(out=tmp, in0=tmp, scalar=-0.5, in1=root, op0=ALU.mult, op1=ALU.mult))
                ch.then(v.scalar_tensor_tensor(out=root, in0=tmp, scalar=1.5, in1=root, op0=ALU.add, op1=ALU.mult))

            dve.sem_inc(tp_free, 2)
            ch.done(v.memset(y_acc[0][:], 0.0))
            ch.done(v.memset(yT_flat[:, KD * HALF:], 0.0))
            ch.done(v.memset(rs[:], 0.0))
            ch.done(v.memset(mv[:], 0.0))
            ch.done(v.memset(tab[:], 0.0))
            ch.done(v.memset(eps_c, EPS))
            ch.done(v.memset(neg_magic, -MAGIC))
            dve.wait_ge(small_in, 32)
            asf, a_w, a_x, a_2 = (scal[:, i:i + 1] for i in range(4))
            ch.done(v.reciprocal(inv_asf, asf))
            ch.done(v.reciprocal(k_x, a_x))
            ch.done(v.reciprocal(k_w, a_w))
            ch.done(v.reciprocal(k_sq, a_2))
            ch.done(v.tensor_scalar(k_sup, a_x, a_w, 1.0 / (ACT_N * WGT_N), ALU.mult, ALU.mult))
            ch.then(v.tensor_scalar(k_out, asf, a_2, 1.0 / ACT_N, ALU.mult, ALU.mult))
            ch.done(v.tensor_scalar(k_x, k_x, ACT_N, None, ALU.mult))
            ch.done(v.tensor_scalar(k_w, k_w, WGT_N, None, ALU.mult))
            ch.then(v.tensor_scalar(k_sq, k_sq, ACT_N, None, ALU.mult))
            dve.sem_inc(scal_ready, 1)
            ch.then(v.tensor_tensor(need_f[:], k_x, k_x, ALU.mult))
            ch.then(v.tensor_scalar(need_f[:], need_f[:], CODE_MAX * CODE_MAX / D, None, ALU.is_gt))
            v.tensor_copy(need_lo[:], need_f[:]).then_inc(need_ready, 1)
            dve.wait_ge(need_ready, 1)
            need = dve.value_load(need_lo[0:1, 0:1], min_val=0, max_val=1)
            def tile_stats(t):
                g, j = t // STEP_A, t % STEP_A
                if j == 0:
                    dve.wait_ge(x_in_sem[g], 16)
                ch.done(v.bn_stats(bn[:, j, :], x[:, t, :]))
                if j == STEP_A - 1:
                    ch.wait()
                    for i in range(STEP_A):
                        last = v.bn_aggr(mv[:, i, :], bn[:, i, :])
                        if i < STEP_A - 1:
                            ch.done(last)
                    last.then_inc(var_ready, 1)

            def row_scales(g):
                dve.wait_ge(var_ready, g + 1)
                ch.wait()
                dve.wait_ge(sd_ready, g + 2 if g else 1)
                a = aff[:, g % 2]
                rsqrt(a, mv[:, :, 1], STEP_A, sd)
                ch.then(v.tensor_scalar(a[:, :, 2], a[:, :, 0], k_x, None, ALU.mult))
                v.scalar_tensor_tensor(out=a[:, :, 3], in0=mv[:, :, 0], scalar=-1.0, in1=a[:, :, 2],
                                       op0=ALU.mult, op1=ALU.mult).then_inc(aff_ready, 1)

            for j in range(STEP_A):
                tile_stats(j)
            dve.wait_ge(w_in_sem, 16)
            for k in range(KD):
                ch.done(v.bn_stats(bn_w[:, k, :], wraw[:, k, :]))
            ch.wait()
            ch.then(v.bn_aggr(mv_w[:, 0, :], bn_w[:].rearrange("p a b -> p (a b)")))
            dve.sem_inc(w_stat_ready, 1)
            row_scales(0)
            dve.wait_ge(stat_mm, 1)
            ch.then(v.tensor_copy(w_mean, stat_ps[:, 0:1]))
            ch.then(v.tensor_scalar(w_off[:], mv_w[:, 0, 0:1], w_mean, None, ALU.subtract))
            ch.then(v.tensor_tensor(w_off[:], w_off[:], w_off[:], ALU.mult))
            ch.then(v.tensor_tensor(mv_w[:, 1, 0:1], w_off[:], mv_w[:, 0, 1:2], ALU.add))
            dve.sem_inc(w_stat_ready, 1)
            dve.wait_ge(sd_ready, 2)
            ch.then(v.reciprocal(w_scale, w_dev[:]))
            ch.then(v.tensor_tensor(w_scale, w_scale, k_w, ALU.mult))
            ch.then(v.tensor_scalar(wraw, wraw, w_mean, w_scale, ALU.subtract, ALU.mult))
            ch.then(v.tensor_scalar(wraw, wraw, WGT_N, -WGT_N, ALU.min, ALU.max))
            v.tensor_scalar(wq, wraw, MAGIC, MAGIC, ALU.add, ALU.subtract).then_inc(wq_ready, 1)

            for t in range(NT + 3):
                nxt = STEP_A * (t // STEP_A + 1)
                if nxt < NT and t % STEP_A == STEP_A - 1:
                    row_scales(nxt // STEP_A)
                if t < NT:
                    dve.wait_ge(xn_ready, t + 1)
                    v.tensor_scalar(q[:, t % 2, :], q[:, t % 2, :], ACT_N, MAGIC, ALU.min, ALU.add) \
                        .then_inc(q_ready, 1)
                if 1 <= t <= NT:
                    dve.wait_ge(qT_hi_ready, t)
                    with dve.If(need > 0):
                        v.scalar_tensor_tensor(out=qT_lo[:, (t - 1) % 2, :], in0=tp[(t - 1) % 2][:], scalar=-MAGIC,
                                               in1=qT_hi[:, (t - 1) % 2, :].bitcast(F32), op0=ALU.add,
                                               op1=ALU.subtract).then_inc(tp_free, 1)
                    with dve.Else():
                        dve.sem_inc(tp_free, 1)
                if t >= 3:
                    u = t - 3
                    dve.wait_ge(sup_ready, u + 1)
                    ch.then(v.tensor_scalar(sup[:, u % 2, :], sup[:, u % 2, :], k_sq, ACT_N, ALU.mult, ALU.min))
                    v.tensor_scalar(S[:, u, :], sup[:, u % 2, :], MAGIC, MAGIC, ALU.add, ALU.subtract) \
                        .then_inc(S_ready, 1)
                if nxt < NT:
                    for j in ((0, 1), (2,), (3,), ())[t % STEP_A]:
                        tile_stats(nxt + j)
                for item, j in first_items(t):
                    split_lo(t - 2 - j, item, j, inv_asf)

            def x1_row(t):
                return x[:, bass.ds(t, 1), :].rearrange("p a n -> p (a n)")

            def post(t, acc):
                dve.wait_ge(acc_full, NT + t + 1)
                xt = x1_row(t)
                v.scalar_tensor_tensor(out=xt, in0=acc[:], scalar=k_out, in1=xt, op0=ALU.mult,
                                       op1=ALU.add).then_inc(x1_ready, 1)
                wait_apart(dve, x1_ready, t + 1, vec_tick)
                ch.done(v.bn_stats(bn[:, 0, :], xt))
                wait_apart(dve, chain_s, ch.base + ch.n, vec_tick)
                v.bn_aggr(mv[:, 0, :], bn[:, 0, :]).then_inc(var_ready, 1)
                dve.wait_ge(var_ready, 4 + t + 1)
                dve.wait_ge(sd_ready, 5 + t + 1)
                rsqrt(rs, mv[:, 0:1, 1], 1, sd)
                if t is not HEAD:
                    dve.wait_ge(tp_full, NT + t)
                v.tensor_scalar(xn1, xt, mv[:, 0, 0:1], rs[:, 0, 0:1], ALU.subtract, ALU.mult) \
                    .then_inc(xn1_ready, 1)

            def group_b(g, last):
                for j in range(4):
                    t = 4 * g + j
                    if not (last and j == 3):
                        for i in range(PIECES):
                            split_lo(PIECES * (t + 3), (j + 3) % RING, i, None if last and j >= 1 else inv_asf)
                    post(t, row_acc[j % 2])
                    if last and j == 1:
                        choose(slice(0, EARLY), 1)
                    if last and j == 2:
                        assign_slots(slice(0, EARLY), 1)

            def next_item(item):
                for i in range(PIECES):
                    split_lo(PIECES * item, item % RING, i, inv_asf)

            dve.wait_ge(consts, 1)
            ch.then(v.tensor_scalar(rev_e[:], iota_r[:, 0:E], -1.0, float(E), ALU.mult, ALU.add))
            mx, km, tot, prob, pos, half, pp, cf, rr, kc, big = (small[:, i, :] for i in range(11))

            def spread(a, ts, n):
                return a[:, ts].unsqueeze(2).to_broadcast([P, ts.stop - ts.start, n])

            def along(a, ts, n):
                return a[:, 0:n].unsqueeze(1).to_broadcast([P, ts.stop - ts.start, n])

            def choose(ts, part):
                dve.wait_ge(gate_done, ts.stop)
                from_gate = (logits if part == 1 else late_logits)[:, ts, :]
                ch.then(v.tensor_reduce(mx[:, ts], from_gate, AX, ALU.max))
                v.tensor_tensor(lgs[:, ts, :], from_gate, spread(mx, ts, E), ALU.subtract) \
                    .then_inc(shift_ready, 1)
                dve.wait_ge(shift_ready, part)
                ch.then(v.scalar_tensor_tensor(out=key[:, ts, :], in0=lgs[:, ts, :], scalar=0.0,
                                               in1=along(rev_e, ts, E), op0=ALU.is_equal, op1=ALU.mult))
                ch.then(v.tensor_reduce(km[:, ts], key[:, ts, :], AX, ALU.max))
                v.tensor_tensor(mask[:, ts, :], key[:, ts, :], spread(km, ts, E), ALU.is_equal).then_inc(mask_ready, 1)

            def assign_slots(ts, part):
                dve.wait_ge(pos_ready, part)
                dve.wait_ge(mask_ready, part)
                p_, h_, pp_, cf_, kc_ = pos[:, ts], half[:, ts], pp[:, ts], cf[:, ts], kc[:, ts]
                before = prefix.rearrange("p (t e) -> p t e", t=NT)
                ch.then(v.tensor_tensor(key[:, ts, :], before[:, ts, :], mask[:, ts, :], ALU.mult))
                ch.then(v.tensor_reduce(p_, key[:, ts, :], AX, ALU.add))
                ch.done(v.tensor_scalar(big[:, ts], p_, float(CAP), 1000.0, ALU.is_ge, ALU.mult))
                ch.then(v.tensor_scalar(h_, p_, float(HALF), None, ALU.is_ge))
                ch.then(v.scalar_tensor_tensor(out=pp_, in0=h_, scalar=-float(HALF), in1=p_, op0=ALU.mult,
                                               op1=ALU.add))
                ch.then(v.tensor_scalar(cf_, pp_, -(P - 1) / 2.0, 1.0 / P, ALU.add, ALU.mult))
                ch.then(v.tensor_scalar(cf_, cf_, MAGIC, MAGIC, ALU.add, ALU.subtract))
                ch.done(v.scalar_tensor_tensor(out=rr[:, ts], in0=cf_, scalar=-float(P), in1=pp_, op0=ALU.mult,
                                               op1=ALU.add))
                ch.then(v.scalar_tensor_tensor(out=kc_, in0=km[:, ts], scalar=-2.0 * NSEG, in1=cf_, op0=ALU.mult,
                                               op1=ALU.add))
                ch.then(v.scalar_tensor_tensor(out=kc_, in0=h_, scalar=float(NSEG), in1=kc_, op0=ALU.mult,
                                               op1=ALU.add))
                ch.then(v.scalar_tensor_tensor(out=kc_, in0=kc_, scalar=float(COLS), in1=big[:, ts], op0=ALU.add,
                                               op1=ALU.add))
                ch.then(v.tensor_tensor(col_hot[:, ts, :], along(iota_r, ts, COLS), spread(kc, ts, COLS),
                                        ALU.is_equal))
                v.tensor_tensor(tok_by_col[:, ts, :], col_hot[:, ts, :], spread(tok1, ts, COLS), ALU.mult) \
                    .then_inc(tok_ready, 1)
                v.tensor_tensor(r_hot[:, ts, :], along(iota_r, ts, P), spread(rr, ts, P), ALU.is_equal) \
                    .then_inc(r_hot_ready, 1)

            next_item(RING)
            dve.wait_ge(acc_full, NT + HEAD)
            for t in range(HEAD):
                v.scalar_tensor_tensor(out=x[:, t, :], in0=y_acc[1 + t][:], scalar=k_out, in1=x[:, t, :],
                                       op0=ALU.mult, op1=ALU.add).then_inc(x1_ready, 1)
            for t in range(HEAD):
                dve.wait_ge(x1_ready, t + 1)
                ch.done(v.bn_stats(bn[:, t, :], x[:, t, :]))
            ch.wait()
            for t in range(HEAD):
                v.bn_aggr(mv[:, t, :], bn[:, t, :]).then_inc(var_ready, 1)
            dve.wait_ge(var_ready, 4 + HEAD)
            dve.wait_ge(sd_ready, 5 + HEAD)
            rsqrt(rs, mv[:, 0:HEAD, 1], HEAD, sd)
            for t in range(HEAD):
                v.tensor_scalar(xn_head[:, t, :], x[:, t, :], mv[:, t, 0:1], rs[:, t, 0:1], ALU.subtract,
                                ALU.mult).then_inc(xn1_ready, 1)
            next_item(RING + 1)
            post(HEAD, row_acc[HEAD % 2])
            next_item(RING + 2)
            per_group = 4 * 5
            start = ch.n
            with dve.Fori(1, 3) as g:
                ch.base, ch.n = (g - 1) * per_group, start
                group_b(g, False)
                assert ch.n == start + per_group, (ch.n - start)
            ch.base, ch.n = 0, start + 2 * per_group
            group_b(3, True)

            choose(slice(EARLY, NT), 2)
            assign_slots(slice(EARLY, NT), 2)
            dve.wait_ge(exp_ready, 1)
            ch.then(v.tensor_reduce(tot, ex[:], AX, ALU.add))
            ch.then(v.reciprocal(prob, tot))
            dve.wait_ge(tok_done, 1)
            ch.then(v.tensor_scalar(empty[:], tok_ps, 0.0, 2.0 * T, ALU.is_equal, ALU.mult))
            v.scalar_tensor_tensor(out=slot_idx[:], in0=tok_ps, scalar=-1.0, in1=empty[:],
                                   op0=ALU.add, op1=ALU.add).then_inc(idx_ready, 1)
            ch.then(v.tensor_tensor(prob_by_col[:, :, 0, :], col_hot, spread(prob, slice(0, NT), COLS), ALU.mult))
            ch.then(v.tensor_tensor(col_hot, col_hot, spread(prob, slice(0, NT), COLS), ALU.mult))
            v.tensor_tensor(prob_by_col[:, :, 1, :], col_hot, prob_by_col[:, :, 0, :].bitcast(F32), ALU.subtract) \
                .then_inc(prob_ready, 1)
            ov, incl, tmp = cnt[:, 1, :], cnt[:, 2, :], cnt[:, 3, :]
            dve.wait_ge(counts_done, 1)
            ch.then(v.tensor_copy(cnt[:, 0, :], counts_ps))
            ch.done(v.tensor_copy(tab[:, 2, 0:E], cnt[:, 0, :]))
            ch.done(v.tensor_copy(tab[:, 0, 0:E], iota_r[:, 0:E]))
            ch.done(v.tensor_scalar(tab[:, 1, 0:E], iota_r[:, 0:E], 2.0 * NSEG, None, ALU.mult))
            ch.done(v.tensor_scalar(ov, cnt[:, 0, :], float(HALF), None, ALU.is_gt))
            ch.then(v.tensor_scalar(incl, cnt[:, 0, :], float(HALF), None, ALU.is_gt))
            for sh in (1, 2, 4):
                ch.then(v.tensor_copy(tmp, incl))
                ch.then(v.tensor_tensor(incl[:, sh:E], tmp[:, sh:E], tmp[:, 0:E - sh], ALU.add))
            ch.then(v.tensor_tensor(tmp, incl, ov, ALU.mult))


            def ln_stats(p, c):
                n = SLOT_TILES[c]
                wait_apart(dve, gathered[c], 16 * (p + 1), vec_tick)
                ch.done(v.bn_stats(bn[0:n, c, :], xg[0:n, c, :]))

            def ln_var_out():
                wait_apart(dve, chain_s, ch.base + ch.n, vec_tick)
                for c, n in enumerate(SLOT_TILES):
                    ch.done(v.bn_aggr(mv[0:n, c, :], bn[0:n, c, :]))
                ch.wait()
                dve.sem_inc(ln_var, 1)

            def ln_scale(p):
                dve.wait_ge(ln_sd, p + 1)
                rsqrt(rs, mv[:, 0:NSEG, 1], NSEG, sd)
                v.scalar_tensor_tensor(out=rs[:, 0:NSEG, 3], in0=mv[:, 0:NSEG, 0], scalar=-1.0,
                                       in1=rs[:, 0:NSEG, 0], op0=ALU.mult, op1=ALU.mult).then_inc(ln_aff, 1)

            LN_CHAIN = 2 * NSEG + 4

            def xT_copy(p, k):
                dve.wait_ge(xt_hi, KD * p + k + 1)
                v.tensor_tensor(xT_lo[:, k, :], tp[(k + 1) % 2][:, 0:HALF], xT_hi[:, k, :].bitcast(F32),
                                ALU.subtract).then_inc(xt_lo, 1)

            def y_copy(p):
                dve.wait_ge(y_done, NF * p)
                for k in range(2, KD):
                    v.tensor_copy(yT[:, k, :], y_acc[k][:, 0:HALF]).then_inc(yt_vec, 1)

            def final(done, cs):
                for c in cs:
                    n = SLOT_TILES[c]
                    dve.wait_ge(fin_full[c], done)
                    dve.wait_ge(rows_kept, NSEG * done)
                    v.scalar_tensor_tensor(out=xres[0:n, c, :], in0=tp[c % 2][0:n, :], scalar=p_s[0:n, c:c + 1],
                                           in1=xres[0:n, c, :], op0=ALU.mult, op1=ALU.add).then_inc(fin_ready[c], 1)

            for c in range(NSEG):
                ln_stats(0, c)
            ln_var_out()
            ln_scale(0)
            dve.wait_ge(ln_aff, 1)
            v.tensor_scalar(xn2[:, 1, :], xg[:, 1, :], mv[:, 1, 0:1], rs[:, 1, 0:1], ALU.subtract, ALU.mult) \
                .then_inc(xn2_ready, 1)
            ch.then(v.tensor_tensor(over[:], tmp.unsqueeze(1).to_broadcast([P, MAX_OVER, E]),
                                    iota_r[:, 1:1 + MAX_OVER].unsqueeze(2).to_broadcast([P, MAX_OVER, E]),
                                    ALU.is_equal))
            ch.then(v.tensor_tensor(over2[:], over[:], iota_r[:, 0:E].unsqueeze(1).to_broadcast([P, MAX_OVER, E]),
                                    ALU.mult))
            ch.then(v.tensor_reduce(tab[:, 0, E:E + MAX_OVER], over2[:], AX, ALU.add))
            ch.then(v.tensor_tensor(over2[:], over[:], cnt[:, 0, :].unsqueeze(1).to_broadcast([P, MAX_OVER, E]),
                                    ALU.mult))
            ch.then(v.tensor_reduce(tab[:, 2, E:E + MAX_OVER], over2[:], AX, ALU.add))
            ch.done(v.tensor_scalar(tab[:, 2, E:E + MAX_OVER], tab[:, 2, E:E + MAX_OVER], -float(HALF), None,
                                    ALU.add))
            ch.done(v.tensor_scalar(tab[:, 1, E:E + MAX_OVER], tab[:, 0, E:E + MAX_OVER], 2.0 * NSEG, float(NSEG),
                                    ALU.mult, ALU.add))
            ch.then(v.tensor_scalar(tab[:, 3, 0:1], incl[:, E - 1:E], float(E), None, ALU.add))
            ch.then(v.tensor_copy(tab_i[:], tab[:]))
            dve.wait_ge(prob_done, 1)
            ch.then(v.tensor_copy(slot_p[:], prob_ps[:, 0:COLS]))
            ch.then(v.tensor_tensor(slot_p[:], prob_ps[:, COLS:2 * COLS], slot_p[:], ALU.add))
            dve.wait_ge(idx_ready, 1)
            dve.sem_inc(tab_ready, 1)
            for k in range(KD):
                xT_copy(0, k)
            n_pass = dve.value_load(tab_i[0:1, 3, 0:1], min_val=E, max_val=E + MAX_OVER)
            start = ch.n
            with dve.Fori(0, n_pass) as p:
                ch.base, ch.n = p * LN_CHAIN, start
                with dve.If(p > 0):
                    y_copy(p)
                with dve.Else():
                    dve.nop()
                for s in range(NF):
                    dve.wait_ge(hh_ready, NF * p + s + 1)
                    v.scalar_tensor_tensor(out=h_lo[:, s % 2, :], in0=row_acc[s % 2][:, 0:HALF], scalar=0.0,
                                           in1=h_hi[:, s % 2, :].bitcast(F32), op0=ALU.max,
                                           op1=ALU.subtract).then_inc(hl_ready, 1)

                    def pieces():
                        for item, js in ring_work(s):
                            for j in js:
                                split_lo(PIECES * (NT + 8 * p + item), item % RING, j)

                    if s in (2, 3):
                        with dve.If(p > 0):
                            final(p, (0, 1) if s == 2 else (2,))
                        with dve.Else():
                            dve.nop()
                    if s < 9:
                        pieces()
                        continue
                    if s < 3 * FC:
                        pieces()
                    with dve.If(p + 1 < n_pass):
                        if s == NF - 1:
                            xT_copy(p + 1, 0)
                            xT_copy(p + 1, 1)
                        if s == 12:
                            ln_scale(p + 1)
                        if s >= 3 * FC:
                            pieces()
                        if s == NF - 1:
                            xT_copy(p + 1, 2)
                            xT_copy(p + 1, 3)
                        if s == 9:
                            ln_stats(p + 1, 0)
                        if s == 10:
                            ln_stats(p + 1, 1)
                            ln_stats(p + 1, 2)
                            ln_var_out()
                    with dve.Else():
                        dve.nop()
                dve.nop()
            y_copy(n_pass)
            final(n_pass, range(NSEG))

        @block.tensor
        def _(pe):
            mm = nc.tensor.matmul
            pe.wait_ge(consts, 1)
            for i in range(2):
                pe.wait_ge(w_stat_ready, i + 1)
                src = mv_w[:, i, 0:1]
                mm(stat_ps[:, i:i + 1], mean_w[:], src, start=True, stop=True).then_inc(stat_mm, 1)
            pe.wait_ge(need_ready, 1)
            need = pe.value_load(need_lo[0:1, 0:1], min_val=0, max_val=1)

            def support(u, parts):
                for k in range(KD):
                    for part in parts:
                        last = mm(row_acc[u % 2][:], part[:, u % 2, k * P:(k + 1) * P], wq[:, k, :],
                                  start=(k == 0 and part is qT_hi), stop=(k == KD - 1 and part is parts[-1]))
                last.then_inc(acc_full, 1)

            def head_rows(u):
                pe.wait_ge(S_ready, u + 1)
                pe.wait_ge(lo_ready, HEAD * (u // PIECES + 1))
                for i in range(HEAD):
                    for part in (hi, lo):
                        last = mm(y_acc[1 + i][:], part[:, i, u * P:(u + 1) * P], S[:, u, :],
                                  start=(u == 0 and part is hi), stop=(u == NT - 1 and part is lo))
                    if u == NT - 1:
                        last.then_inc(acc_full, 1)

            for t in range(NT + 1):
                if t < NT:
                    pe.wait_ge(q_ready, t + 1)
                    pe.wait_ge(tp_free, t + 1)
                    for k in range(KD):
                        last = nc.tensor.transpose(tp[t % 2][:, k * P:(k + 1) * P],
                                                   q[:, t % 2, k * P:(k + 1) * P], ident[:])
                    last.then_inc(tp_full, 1)
                if t == 1:
                    pe.wait_ge(wq_ready, 1)
                if t >= 1:
                    u = t - 1
                    pe.wait_ge(tp_free, 2 + u + 1)
                    if u >= 2:
                        pe.wait_ge(sup_ready, u - 1)
                    with pe.If(need > 0):
                        support(u, (qT_hi, qT_lo))
                    with pe.Else():
                        support(u, (qT_hi,))
                if t >= HEAD_LAG:
                    head_rows(t - HEAD_LAG)
            for u in range(NT + 1 - HEAD_LAG, NT):
                head_rows(u)

            def gate_in(step, b, rows=xn1):
                pe.wait_ge(xn1_ready, step)
                for k in range(KD):
                    last = nc.tensor.transpose(tp[b][:, k * P:(k + 1) * P], rows[:, k * P:(k + 1) * P], ident[:])
                last.then_inc(tp_full, 1)

            def gate_out(step):
                pe.wait_ge(xn1T_ready, step)
                late = isinstance(step, int) and step > EARLY
                dst = (late_cols if late else logit_cols)[:, bass.ds(step, 1), :].rearrange("p a e -> p (a e)")
                for k in range(KD):
                    last = mm(dst, xn1T[:, k, :], gate[:, k, :], start=(k == 0), stop=(k == KD - 1))
                last.then_inc(gate_done, 1)

            def adj_rows(t, j, jts, stop):
                for jt in jts:
                    for part in (hi, lo):
                        last = mm(row_acc[j % 2][:], part[:, j, jt * P:(jt + 1) * P], S[:, jt, :],
                                  start=(jt == 0 and part is hi), stop=(jt == NT - 1 and part is lo))
                if stop:
                    last.then_inc(acc_full, 1)

            def tile(t, j):
                adj_rows(t, j, range(10), False)
                gate_in(t, (j - 1) % 2)
                adj_rows(t, j, range(10, NT), True)
                gate_out(t)

            def tile_and_head_gates(t):
                adj_rows(t, 0, range(4), False)
                for step in range(1, HEAD + 1):
                    gate_in(step, (step - 1) % 2, xn_head[:, step - 1, :])
                    adj_rows(t, 0, range(2 + 2 * step, 4 + 2 * step), False)
                    gate_out(step)
                adj_rows(t, 0, range(10, 14), False)
                gate_in(HEAD + 1, 1)
                adj_rows(t, 0, range(14, NT), True)
                gate_out(HEAD + 1)

            def group_b(g, last):
                for j in range(4):
                    t = 4 * g + j
                    pe.wait_ge(lo_ready, PIECES * (t + 1))
                    if j == 0 and not last:
                        with pe.If(g > 1):
                            tile(t, j)
                        with pe.Else():
                            tile_and_head_gates(t)
                    else:
                        tile(t, j)
                    if last and j == 2:
                        choices(slice(0, EARLY), 1)
                    if last and j == 3:
                        tokens(slice(0, EARLY), 1)

            mflat = mask[:].rearrange("p t e -> p (t e)")

            def choices(ts, part):
                pe.wait_ge(mask_ready, part)
                mm(prefix[:, ts.start * E:ts.stop * E], tri[:], mflat[:, ts.start * E:ts.stop * E], start=True,
                   stop=False)
                for sh in range(1, ts.stop):
                    a = max(ts.start, sh)
                    last = mm(prefix[:, a * E:ts.stop * E], ones_b[:], mflat[:, (a - sh) * E:(ts.stop - sh) * E],
                              start=False, stop=(sh == ts.stop - 1))
                last.then_inc(pos_ready, 1)

            def tokens(ts, part):
                pe.wait_ge(tok_ready, part)
                pe.wait_ge(r_hot_ready, part)
                for t in range(ts.start, ts.stop):
                    last = mm(tok_ps, r_hot[:, t, :], tok_by_col[:, t, :], start=(t == 0), stop=(t == NT - 1))
                if ts.stop == NT:
                    last.then_inc(tok_done, 1)

            pe.wait_ge(lo_ready, PIECES * RING)
            adj_rows(HEAD, HEAD, range(NT), True)
            with pe.Fori(1, 3) as g:
                group_b(g, False)
            group_b(3, True)
            gate_in(NT, 1)
            gate_out(NT)

            choices(slice(EARLY, NT), 2)
            for t in range(NT):
                last = mm(counts_ps, ones_b[:], mask[:, t, :], start=(t == 0), stop=(t == NT - 1))
            last.then_inc(counts_done, 1)
            tokens(slice(EARLY, NT), 2)
            pe.wait_ge(prob_ready, 1)
            for t in range(NT):
                last = mm(prob_ps, r_hot[:, t, :], prob_by_col[:, t, :, :].rearrange("p j c -> p (j c)"),
                          start=(t == 0), stop=(t == NT - 1))
            last.then_inc(prob_done, 1)


            def xT(p, k):
                pe.wait_ge(xn2_ready, NSEG * (p + 1))
                if k >= 2:
                    pe.wait_ge(xt_lo, KD * p + k - 1)
                at = 0
                for c, n in enumerate(SLOT_TILES):
                    last = nc.tensor.transpose(tp[(k + 1) % 2][:, at:at + n], xn2[0:n, c, k * P:(k + 1) * P],
                                               ident[0:n, 0:n])
                    at += n
                last.then_inc(xt_full, 1)

            def final(done, c):
                if c == 0:
                    pe.wait_ge(yt_act, 2 * done)
                    pe.wait_ge(yt_vec, 2 * done)
                if c >= 2:
                    pe.wait_ge(fin_ready[c - 2], done)
                for k in range(KD):
                    at = k * HALF + c * P
                    last = nc.tensor.transpose(tp[c % 2][:, k * P:(k + 1) * P], yT_flat[:, at:at + P], ident[:])
                last.then_inc(fin_full[c], 1)

            def up(p, s, w):
                item = 2 * (s // FC)
                if s % FC == 0:
                    pe.wait_ge(lo_ready, PIECES * (NT + 8 * p + item + 1))
                if s >= 2:
                    pe.wait_ge(hl_ready, NF * p + s - 1)
                for k in range(KD):
                    if s == 0:
                        pe.wait_ge(xt_lo, KD * p + k + 1)
                    at = k * FC * P + (s % FC) * P
                    for i, (a, b) in enumerate(((hi, xT_hi), (hi, xT_lo), (lo, xT_hi))):
                        last = mm(row_acc[s % 2][:, 0:w], a[:, item % RING, at:at + P], b[:, k, 0:w],
                                  start=(k == 0 and i == 0), stop=(k == KD - 1 and i == 2))
                last.then_inc(h_full, 1)

            def down(p, s, w):
                item = 2 * (s // FC) + 1
                if s % FC == 0:
                    pe.wait_ge(lo_ready, PIECES * (NT + 8 * p + item + 1))
                pe.wait_ge(hl_ready, NF * p + s + 1)
                for k in range(KD):
                    at = (s % FC) * D + k * P
                    for i, (a, b) in enumerate(((hi, h_hi), (hi, h_lo), (lo, h_hi))):
                        last = mm(y_acc[k][:, 0:w], a[:, item % RING, at:at + P], b[:, s % 2, 0:w],
                                  start=(s == 0 and i == 0), stop=(s == NF - 1 and i == 2))
                last.then_inc(y_done, 1)

            def expert_pass(p, w):
                for s in range(NF):
                    if s == NF - 1:
                        with pe.If(p + 1 < n_pass):
                            pe.wait_ge(rotated, 2 * NSEG * (p + 1))
                            xT(p + 1, 0)
                            xT(p + 1, 1)
                        with pe.Else():
                            pe.nop()
                    up(p, s, w)
                    if s in (1, 2, 3):
                        with pe.If(p > 0):
                            if s == 1:
                                pe.wait_ge(yt_act, 2 * p)
                                pe.wait_ge(yt_vec, 2 * p)
                                pe.nop()
                            for c in {1: (), 2: (0, 1), 3: (2,)}[s]:
                                final(p, c)
                        with pe.Else():
                            pe.nop()
                    if s >= 1:
                        down(p, s - 1, w)
                down(p, NF - 1, w)
                with pe.If(p + 1 < n_pass):
                    xT(p + 1, 2)
                    xT(p + 1, 3)
                with pe.Else():
                    pe.nop()

            for k in range(KD):
                xT(0, k)
            pe.wait_ge(tab_ready, 1)
            n_pass = pe.value_load(tab_i[0:1, 3, 0:1], min_val=E, max_val=E + MAX_OVER)
            with pe.Fori(0, n_pass) as p:
                n_tok = pe.value_load(tab_i[0:1, 2, bass.ds(p, 1)])

                def narrowest(i):
                    if i == len(WIDTHS) - 1:
                        expert_pass(p, WIDTHS[i])
                        return
                    with pe.If(n_tok <= WIDTHS[i]):
                        expert_pass(p, WIDTHS[i])
                    with pe.Else():
                        narrowest(i + 1)
                    pe.nop()

                narrowest(0)
            for c in range(NSEG):
                final(n_pass, c)


def kernel(**inputs):
    import numpy as np
    import concourse.bacc as bacc
    from concourse import mybir as mb
    from concourse.bass_utils import run_bass_kernel_spmd

    f = {k: np.asarray(a) for k, a in inputs.items()}
    arrays = {
        "x_rows": f["x"].reshape(NT, P, D).transpose(1, 0, 2),
        "adj_tiles": f["adj"].reshape(NT, P, NT, P).transpose(0, 3, 2, 1).reshape(NT, P, ITEM),
        "gnn_weight": f["L0_gnn_weight"].reshape(KD, P, D).transpose(1, 0, 2),
        "scales": np.broadcast_to(np.stack([f["L0_gnn_" + k].reshape(()) for k in (
            "adj_scaling_factor", "wgt_alpha", "act_alpha", "act_alpha2", "act_alpha2")]), (P, 5)),
        "gate_w": f["L0_ffn_gate_w"].reshape(KD, P, E).transpose(1, 0, 2),
        "experts": np.stack([
            f["L0_ffn_w1"].reshape(E, KD, P, NC, FC * P).transpose(0, 3, 2, 1, 4).reshape(E, NC, P, ITEM),
            f["L0_ffn_w2"].reshape(E, NC, FC, P, D).transpose(0, 1, 3, 2, 4).reshape(E, NC, P, ITEM),
        ], axis=2).reshape(E * NC * 2, P, ITEM),
    }
    arrays = {k: np.ascontiguousarray(a) for k, a in arrays.items()}
    nc = bacc.Bacc("TRN2", target_bir_lowering=False, num_devices=1)
    ins = [nc.dram_tensor(k, a.shape, mb.dt.from_np(a.dtype), kind="ExternalInput").ap()
           for k, a in arrays.items()]
    out = nc.dram_tensor("out_rows", (T, D), mb.dt.float32, kind="ExternalOutput").ap()
    x1_rows = nc.dram_tensor("x1_rows", (T, D), mb.dt.float32, kind="Internal").ap()
    gnn_moe_kernel(nc, ins[0], ins[1], ins[2], ins[3], ins[4], ins[5], out, x1_rows)
    r = run_bass_kernel_spmd(nc, [arrays], core_ids=[0])
    return r.results[0]["out_rows"]
```
